# Optimizing a Trainium2 kernel written in Bass

```python
import numpy as np
import jax
import jax.numpy as jnp

def _softmax(x, axis=-1):
    return jax.nn.softmax(x, axis=axis)

def _gelu(x):
    return jax.nn.gelu(x, approximate=True)

def _silu(x):
    return jax.nn.silu(x)

def _sigmoid(x):
    return jax.nn.sigmoid(x)

def _layernorm(x, axis=-1, eps=1e-05):
    m = jnp.mean(x, axis=axis, keepdims=True)
    v = jnp.var(x, axis=axis, keepdims=True)
    return (x - m) / jnp.sqrt(v + eps)

def _scatter_add(tgt, idx, src, axis=0):
    return tgt.at[idx].add(src)

def _segment_sum(src, seg, n):
    return jax.ops.segment_sum(src, seg, n)
kernel_name = 'mk_sandwich_d1_jaxref_r8_426251'

def setup_inputs(seed: int=0):
    np.random.seed(seed)
    _w = jnp.asarray

    def _L0_attn_setup():
        import jax, jax.numpy as jnp
        import numpy as np
        B, S, D, H = (1, 512, 128, 16)
        DH = D // H

        def _positional_encoding(seq_len, d_model, dtype):
            pos = jnp.arange(seq_len, dtype=dtype)[:, None]
            div = jnp.exp(jnp.arange(0, d_model, 2, dtype=dtype) * (-np.log(10000.0) / d_model))
            pe = jnp.zeros((seq_len, d_model), dtype=dtype)
            pe = pe.at[:, 0::2].set(jnp.sin(pos * div))
            pe = pe.at[:, 1::2].set(jnp.cos(pos * div))
            return pe
        key = jax.random.key(seed)
        ks = jax.random.split(key, 11)
        s = 1.0 / np.sqrt(D)
        return {'x': jax.random.normal(ks[0], (B, S, D), dtype=jnp.float32), 'Wq': jax.random.normal(ks[1], (D, D), dtype=jnp.float32) * s, 'bq': jnp.zeros((D,), dtype=jnp.float32), 'Wk': jax.random.normal(ks[2], (D, D), dtype=jnp.float32) * s, 'bk': jnp.zeros((D,), dtype=jnp.float32), 'Wv': jax.random.normal(ks[3], (D, D), dtype=jnp.float32) * s, 'bv': jnp.zeros((D,), dtype=jnp.float32), 'Wo': jax.random.normal(ks[4], (D, D), dtype=jnp.float32) * s, 'bo': jnp.zeros((D,), dtype=jnp.float32), 'gamma': jnp.ones((D,), dtype=jnp.float32), 'beta': jnp.zeros((D,), dtype=jnp.float32)}
    _L0_attn_in = _L0_attn_setup()

    def _L0_ffn_setup():
        import jax, jax.numpy as jnp
        import numpy as np
        CAPACITY = 2
        B, S, D, E, I = (4, 512, 128, 8, 512)
        key = jax.random.key(seed)
        k0, k1, k2, k3, k4 = jax.random.split(key, 5)
        x = jax.random.normal(k0, (B, S, D), dtype=jnp.float32)
        gate_w = jax.random.normal(k1, (E, D), dtype=jnp.float32) * 0.006
        w_gate = jax.random.normal(k2, (E, I, D), dtype=jnp.float32) * (1.0 / np.sqrt(D))
        w_up = jax.random.normal(k3, (E, I, D), dtype=jnp.float32) * (1.0 / np.sqrt(D))
        w_down = jax.random.normal(k4, (E, D, I), dtype=jnp.float32) * (1.0 / np.sqrt(I))
        return {'x': x, 'gate_w': gate_w, 'w_gate': w_gate, 'w_up': w_up, 'w_down': w_down}
    _L0_ffn_in = _L0_ffn_setup()
    _d = {'L0_attn_x': _L0_attn_in['x'], 'L0_attn_Wq': _L0_attn_in['Wq'], 'L0_attn_bq': _L0_attn_in['bq'], 'L0_attn_Wk': _L0_attn_in['Wk'], 'L0_attn_bk': _L0_attn_in['bk'], 'L0_attn_Wv': _L0_attn_in['Wv'], 'L0_attn_bv': _L0_attn_in['bv'], 'L0_attn_Wo': _L0_attn_in['Wo'], 'L0_attn_bo': _L0_attn_in['bo'], 'L0_attn_gamma': _L0_attn_in['gamma'], 'L0_attn_beta': _L0_attn_in['beta'], 'L0_ffn_gate_w': _L0_ffn_in['gate_w'], 'L0_ffn_w_gate': _L0_ffn_in['w_gate'], 'L0_ffn_w_up': _L0_ffn_in['w_up'], 'L0_ffn_w_down': _L0_ffn_in['w_down']}
    _x0 = _d['L0_attn_x']
    _d['L0_attn_x'] = jax.random.normal(jax.random.fold_in(jax.random.key(seed), 1), (32, 256, 128), dtype=_x0.dtype)
    del _x0
    return _d

def reference(L0_attn_x, L0_attn_Wq, L0_attn_bq, L0_attn_Wk, L0_attn_bk, L0_attn_Wv, L0_attn_bv, L0_attn_Wo, L0_attn_bo, L0_attn_gamma, L0_attn_beta, L0_ffn_gate_w, L0_ffn_w_gate, L0_ffn_w_up, L0_ffn_w_down):

    def _L0_attn_ref(x, Wq, bq, Wk, bk, Wv, bv, Wo, bo, gamma, beta):
        import jax, jax.numpy as jnp
        import numpy as np
        B, S, D, H = (1, 512, 128, 16)
        DH = D // H

        def _positional_encoding(seq_len, d_model, dtype):
            pos = jnp.arange(seq_len, dtype=dtype)[:, None]
            div = jnp.exp(jnp.arange(0, d_model, 2, dtype=dtype) * (-np.log(10000.0) / d_model))
            pe = jnp.zeros((seq_len, d_model), dtype=dtype)
            pe = pe.at[:, 0::2].set(jnp.sin(pos * div))
            pe = pe.at[:, 1::2].set(jnp.cos(pos * div))
            return pe
        b, s, d = x.shape
        h = x + _positional_encoding(s, d, x.dtype)[None, :, :]
        q = (h @ Wq + bq).reshape(b, s, H, DH)
        k = (h @ Wk + bk).reshape(b, s, H, DH)
        v = (h @ Wv + bv).reshape(b, s, H, DH)
        scores = jnp.einsum('bshd,bthd->bhst', q, k) / np.sqrt(DH)
        attn = jax.nn.softmax(scores, axis=-1)
        out = jnp.einsum('bhst,bthd->bshd', attn, v).reshape(b, s, d)
        out = out @ Wo + bo
        y = h + out
        mu = jnp.mean(y, axis=-1, keepdims=True)
        var = jnp.var(y, axis=-1, keepdims=True)
        return (y - mu) * jax.lax.rsqrt(var + 1e-05) * gamma + beta

    def _L0_ffn_ref(x, gate_w, w_gate, w_up, w_down):
        import jax, jax.numpy as jnp
        import numpy as np
        CAPACITY = 2
        B, S, D = x.shape
        E = gate_w.shape[0]
        k = S // E * CAPACITY
        logits = jnp.einsum('bsd,ed->bse', x, gate_w)
        affinity = jax.nn.softmax(logits, axis=-1)
        affinity = jnp.transpose(affinity, (0, 2, 1))
        gating, idx = jax.lax.top_k(affinity, k)
        bidx = jnp.arange(B)[:, None, None]
        x_in = x[bidx, idx]
        h = jax.nn.silu(jnp.einsum('bekd,eid->beki', x_in, w_gate)) * jnp.einsum('bekd,eid->beki', x_in, w_up)
        x_e = jnp.einsum('beki,edi->bekd', h, w_down)
        out = jnp.zeros_like(x).at[bidx, idx].add(gating[..., None] * x_e)
        return out
    x = L0_attn_x
    x = x + _layernorm(_L0_attn_ref(_layernorm(x, axis=-1), L0_attn_Wq, L0_attn_bq, L0_attn_Wk, L0_attn_bk, L0_attn_Wv, L0_attn_bv, L0_attn_Wo, L0_attn_bo, L0_attn_gamma, L0_attn_beta), axis=-1)
    x = x + _layernorm(_L0_ffn_ref(_layernorm(x, axis=-1), L0_ffn_gate_w, L0_ffn_w_gate, L0_ffn_w_up, L0_ffn_w_down), axis=-1)
    return x

_drawn_inputs = setup_inputs


def setup_inputs(seed=0):
    import zlib

    import numpy as np

    out = dict(_drawn_inputs(seed))
    spreads = {'L0_attn_bq': (0.0, 0.1),
     'L0_attn_bk': (0.0, 0.1),
     'L0_attn_bv': (0.0, 0.1),
     'L0_attn_bo': (0.0, 0.1),
     'L0_attn_gamma': (1.0, 0.2),
     'L0_attn_beta': (0.0, 0.1)}
    factors = {}
    for name, (base, spread) in spreads.items():
        noise = np.random.default_rng([zlib.crc32(name.encode()), seed]).standard_normal(out[name].shape)
        drawn = base * np.exp(spread * noise) if base else spread * noise
        out[name] = jnp.asarray(drawn.astype(out[name].dtype))
    for name, factor in factors.items():
        out[name] = (out[name] * factor).astype(out[name].dtype)
    return out
```

```python
import concourse.bass as bass
from concourse import mybir
from contextlib import ExitStack

B, S, D, H, E, I = 32, 256, 128, 16, 8, 512
DH = D // H
CAP = S // E * 2
P = 128
ST = S // P
IT = I // P
EPS = 1e-5
SCALE = float(DH) ** -0.5

QPART = (0, 0, 0, 1, 1, 2)
KPART = (0, 1, 2, 0, 1, 0)
NPROD = len(QPART)
MROW = 96
KROWS = MROW + 3

NB4 = 4
LOOP0, NLOOP = 2, 6
FIRST, LAST = -3, B + 1
GB = 8
NG = B // GB
M = E // 2


def add(q, k):
    return q + k if k else q


def live(q, c):
    return not isinstance(q, int) or 0 <= 4 * q + c < B


def has_prior(q, c, n):
    return not isinstance(q, int) or 4 * q + c >= n


def batch(q, c, d):
    return add(q, (c + d) // 4), (c + d) % 4


def nth(q, c, k, m):
    return add(4 * k * q, k * c + m)


MISC = (("OT", -1), ("onT", -1), ("hT", 3), ("Wo", -1), ("QK", 3), ("V", 3), ("nmT", 1), ("xnT", -2), ("logit", -2))


def misc_use(q, c, name):
    if not isinstance(q, int):
        return add(4 * len(MISC) * q, len(MISC) * (c - LOOP0) + misc_use(0, LOOP0, name))
    s, n = 4 * q + c, 0
    for t in range(FIRST, s + 1):
        for use, d in MISC:
            if t == s and use == name:
                return n
            n += 0 <= t + d < B
    raise ValueError(name)


def build(nc, x, Wq, bq, Wk, bk, Wv, bv, Wo, bo, gamma, beta, gate, wg, wu, wd, pe_tab, out):
    F32, BF16, U32 = mybir.dt.float32, mybir.dt.bfloat16, mybir.dt.uint32
    ALU, ACT, AX = mybir.AluOpType, mybir.ActivationFunctionType, mybir.AxisListType
    top = ExitStack()
    names = [0]

    def sem(name):
        return top.enter_context(nc.semaphore(name))

    def steps(eng, run):
        for s in range(FIRST, LOOP0):
            run(s // 4, s % 4)
        with eng.Fori(0, NLOOP) as g:
            for j in range(4):
                run(add(g, (LOOP0 + j) // 4), (LOOP0 + j) % 4)
        for s in range(LOOP0 + 4 * NLOOP, LAST + 1):
            run(s // 4, s % 4)

    with top:
        def sb(name, shape, dt=F32, ctx=top):
            return ctx.enter_context(nc.sbuf_tensor(name, shape, dt))

        def ps(name, shape, dt=F32, ctx=top):
            return ctx.enter_context(nc.psum_tensor(name, shape, dt))

        x1_dram = nc.dram_tensor("x1_scratch", (B, P, ST, D), F32, kind="Internal").ap()
        xn_dram = nc.dram_tensor("xn_scratch", (B, P, ST, D), F32, kind="Internal").ap()

        wg_sb = sb("wg_sb", [P, E, I])
        wu_sb = sb("wu_sb", [P, E, I])
        wd_sb = sb("wd_sb", [P, E, IT, D])
        ident = sb("ident", [P, P])
        identb = sb("identb", [P, P], BF16)
        logits = sb("logits", [P, ST, B, E])
        slot_token = sb("slot_token", [P, B, M])
        slot_gate = sb("slot_gate", [P, B, M])
        neghalf = sb("neghalf", [P, ST])
        w_loaded = sem("w_loaded")
        consts = sem("consts")
        carried = sem("carried")

        def settled(eng):
            eng.sem_inc(carried, 1)


        with ExitStack() as actx:
            def sa(name, shape, dt=F32):
                return sb(name, shape, dt, actx)

            qs = sa("qs", [P, NB4, H, S], BF16)
            ks = sa("ks", [P, NB4, H, S], BF16)
            vst = sa("vst", [P, NB4, ST, H, 32])
            probs = sa("probs", [P, 4, 4, S])
            h_bo = sa("h_bo", [P, NB4, ST, D])
            x_in = sa("x_in", [P, 2, ST, D])
            x_res = sa("x_res", [P, 2, ST, D])
            xn1 = sa("xn1", [P, 2, ST, D])
            h = sa("h", [P, 2, ST, D])
            hT = sa("hT", [P, S])
            qk_part = sa("qk_part", [P, 3, 2, S], BF16)
            qk_rest = sa("qk_rest", [P, 2, S])
            nm = sa("nm", [P, 2, ST, H])
            nm_part = sa("nm_part", [P, ST, 3, H], BF16)
            nm_rest = sa("nm_rest", [P, ST, H])
            nmT = sa("nmT", [3 * H, S], BF16)
            o_aug = sa("o_aug", [P, 2, S])
            o_rec = sa("o_rec", [P, ST * H])
            o_norm = sa("o_norm", [P, ST, D])
            onT = sa("onT", [P, S])
            y = sa("y", [P, ST, D])
            z2 = sa("z2", [P, ST, D])
            z2g = sa("z2g", [P, ST, D])
            z2b = sa("z2b", [P, ST, D])
            z3 = sa("z3", [P, ST, D])
            x1 = sa("x1", [P, 2, ST, D])
            xn2 = sa("xn2", [P, 2, ST, D])
            xnT = sa("xnT", [P, S])
            stats = [sa(f"stats{n}", [P, ST, 6]) for n in range(4)]
            mv = [sa(f"mv{n}", [P, ST, 2]) for n in range(4)]
            veps = [sa(f"veps{n}", [P, ST]) for n in range(4)]
            rstd = [sa(f"rstd{n}", [P, ST]) for n in range(4)]
            wq_sb, wk_sb, wv_sb, wo_sb = (sa(n, [P, D]) for n in ("wq_sb", "wk_sb", "wv_sb", "wo_sb"))
            gate_sb = sa("gate_sb", [P, E])
            bq_sb, bk_sb = sa("bq_sb", [P, 1]), sa("bk_sb", [P, 1])
            bv_sb, bo_sb, gam_sb, bet_sb = (sa(n, [P, D]) for n in ("bv_sb", "bo_sb", "gam_sb", "bet_sb"))
            pe_sb = sa("pe_sb", [P, ST, D])
            pebo = sa("pebo", [P, ST, D])

            ps_s = [ps(f"ps_s{n}", [P, 2, S], F32, actx) for n in range(2)]
            ps_st = [ps(f"ps_st{n}", [P, 4, S], F32, actx) for n in range(2)]
            ps_av = ps("ps_av", [P, 2, S], F32, actx)
            misc = ps("misc", [P, 512], F32, actx)

            small_loaded = sem("small_loaded")
            x_loaded = [sem(f"x_loaded{n}") for n in range(2)]
            res_loaded = [sem(f"res_loaded{n}") for n in range(2)]
            spread = [sem(f"spread{n}") for n in range(NB4)]
            nm_spread = [sem(f"nm_spread{n}") for n in range(NB4)]
            x1_stored = [sem(f"x1_stored{n}") for n in range(2)]
            xn_stored = [sem(f"xn_stored{n}") for n in range(2)]
            misc_full, misc_free = sem("misc_full"), sem("misc_free")
            s_done, max_done = sem("s_done"), sem("max_done")
            st_done, exp_done, av_done = sem("st_done"), sem("exp_done"), sem("av_done")
            oaug_done, orec_done = sem("oaug_done"), sem("orec_done")
            stats_done = [sem(f"stats_done{n}") for n in range(4)]
            mv_done = [sem(f"mv_done{n}") for n in range(4)]
            veps_done = [sem(f"veps_done{n}") for n in range(4)]
            rstd_done = [sem(f"rstd_done{n}") for n in range(4)]
            norm_done = [sem(f"norm_done{n}") for n in range(4)]
            h_done, hbo_done = sem("h_done"), sem("hbo_done")
            part0_done, rest_done, part1_done, part2_done = (sem(f"qk{n}_done") for n in range(4))
            v_done = sem("v_done")
            nm0_done, nmr_done, nm1_done, nm2_done = (sem(f"nm{n}_done") for n in range(4))
            gam_done, bet_done, x1_done = sem("gam_done"), sem("bet_done"), sem("x1_done")
            pebo_done = sem("pebo_done")
            NSMALL = 12

            def x_rows(src, q, c):
                if isinstance(q, int):
                    v = src[4 * q + c:4 * q + c + 1]
                else:
                    v = src[bass.ds(add(4 * q, c), 1)]
                return v.rearrange("b (t p) d -> (b p) t d", p=P)

            def scratch(dst, q, c):
                if isinstance(q, int):
                    v = dst[4 * q + c:4 * q + c + 1]
                else:
                    v = dst[bass.ds(add(4 * q, c), 1)]
                return v.rearrange("b p t d -> (b p) t d")

            with nc.Block() as block:
                @block.sync
                def _(sp):
                    sp.dma_start(x_in[:, 0], x_rows(x, 0, 0)).then_inc(x_loaded[0], 16)
                    for dst, src in ((wq_sb, Wq), (wk_sb, Wk), (wv_sb, Wv), (wo_sb, Wo), (gate_sb, gate)):
                        sp.dma_start(dst[:], src).then_inc(small_loaded, 16)
                    for dst, src in ((bq_sb, bq), (bk_sb, bk)):
                        sp.dma_start(dst[:], src.rearrange("(d a) -> d a", a=1)).then_inc(small_loaded, 16)
                    for dst, src in ((bv_sb, bv), (bo_sb, bo), (gam_sb, gamma), (bet_sb, beta)):
                        sp.dma_start(dst[:], src.rearrange("(a d) -> a d", a=1).broadcast_to([P, D])).then_inc(small_loaded, 16)
                    sp.dma_start(pe_sb[:], pe_tab.rearrange("(t p) d -> p t d", p=P)).then_inc(small_loaded, 16)

                    def run(q, c):
                        b4, c4 = batch(q, c, 4)
                        if live(b4, c4):
                            if has_prior(b4, c4, 2):
                                sp.wait_ge(norm_done[0], nth(b4, c4, 2, -2))
                            settled(sp)
                            sp.dma_start(x_in[:, c4 % 2], x_rows(x, b4, c4)).then_inc(x_loaded[c4 % 2], 16)
                        b, cc = batch(q, c, -1)
                        if live(b, cc):
                            if has_prior(b, cc, 2):
                                sp.wait_ge(x1_done, nth(b, cc, 1, -1))
                            settled(sp)
                            sp.dma_start(x_res[:, cc % 2], x_rows(x, b, cc)).then_inc(res_loaded[cc % 2], 16)
                        b, cc = batch(q, c, -2)
                        if live(b, cc):
                            sp.wait_ge(x1_done, nth(b, cc, 1, 1))
                            settled(sp)
                            sp.dma_start(scratch(x1_dram, b, cc), x1[:, cc % 2]).then_inc(x1_stored[cc % 2], 16)
                            sp.wait_ge(norm_done[3], nth(b, cc, 2, 2))
                            settled(sp)
                            sp.dma_start(scratch(xn_dram, b, cc), xn2[:, cc % 2]).then_inc(xn_stored[cc % 2], 16)
                        b, cc = batch(q, c, 3)
                        if live(b, cc):
                            if has_prior(b, cc, 4):
                                sp.wait_ge(st_done, nth(b, cc, 8, -24))
                                settled(sp)
                            else:
                                sp.wait_ge(consts, 7)
                            sp.wait_ge(part0_done, nth(b, cc, 2, 2))
                            settled(sp)
                            sp.wait_ge(part1_done, nth(b, cc, 1, 1))
                            settled(sp)
                            sp.wait_ge(part2_done, nth(b, cc, 1, 1))
                            for rows, side, parts in ((qs, 0, QPART), (ks, 1, KPART)):
                                for n, part in enumerate(parts):
                                    sp.dma_start(rows[n * DH:(n + 1) * DH, cc], qk_part[:, part, side]
                                                 ).then_inc(spread[cc], 16)
                        b, cc = batch(q, c, 1)
                        if live(b, cc):
                            sp.wait_ge(misc_free, add(misc_use(q, c, "nmT"), 1))
                            sp.dma_start(qs[MROW:MROW + 3, cc], nmT[:]).then_inc(nm_spread[cc], 16)

                    steps(sp, run)
                    for n in range(2):
                        sp.wait_ge(x1_stored[n], 16 * (B // 2))
                        sp.wait_ge(xn_stored[n], 16 * (B // 2))

                @block.gpsimd
                def _(pool):
                    pool.memset(ident[:], 0.0).then_inc(consts, 1)
                    pool.memset(identb[:], 0.0).then_inc(consts, 1)
                    pool.memset(neghalf[:], -0.5).then_inc(consts, 1)
                    pool.wait_ge(consts, 5)
                    for m in (ident, identb):
                        pool.affine_select(out=m[:], in_=m[:], compare_op=ALU.not_equal, fill=1.0, base=0,
                                           pattern=[[-1, P]], channel_multiplier=1).then_inc(consts, 1)
                    pool.wait_ge(small_loaded, 16 * NSMALL)
                    for t in range(ST):
                        pool.tensor_tensor(out=pebo[:, t], in0=pe_sb[:, t], in1=bo_sb[:], op=ALU.add).then_inc(pebo_done, 1)
                    pool.wait_ge(pebo_done, ST)

                    def rsqrt(n, b, c):
                        pool.wait_ge(mv_done[n], nth(b, c, 2, 2))
                        settled(pool)
                        pool.tensor_scalar(out=veps[n][:], in0=mv[n][:, :, 1], scalar1=EPS, scalar2=None, op0=ALU.add
                                           ).then_inc(veps_done[n], 1)
                        pool.wait_ge(veps_done[n], nth(b, c, 1, 1))
                        if has_prior(b, c, 1):
                            pool.wait_ge(norm_done[n], nth(b, c, 2, 0))
                        pool.tensor_tensor(out=rstd[n][:], in0=veps[n][:], in1=neghalf[:], op=ALU.pow
                                           ).then_inc(rstd_done[n], 1)

                    def run(q, c):
                        b, cc = batch(q, c, 3)
                        if live(b, cc):
                            rsqrt(0, b, cc)
                        b2, c2 = batch(q, c, -2)
                        if live(b2, c2):
                            rsqrt(3, b2, c2)
                        if live(b, cc):
                            pool.wait_ge(norm_done[0], nth(b, cc, 2, 2))
                            if has_prior(b, cc, 2):
                                pool.wait_ge(part0_done, nth(b, cc, 2, -2))
                            pool.tensor_tensor(out=h[:, cc % 2], in0=xn1[:, cc % 2], in1=pe_sb[:], op=ALU.add
                                               ).then_inc(h_done, 1)
                        b1, c1 = batch(q, c, -1)
                        if live(b1, c1):
                            rsqrt(1, b1, c1)
                        if live(b, cc):
                            if has_prior(b, cc, 4):
                                pool.wait_ge(stats_done[1], nth(b, cc, 2, -6))
                            pool.tensor_tensor(out=h_bo[:, cc], in0=xn1[:, cc % 2], in1=pebo[:], op=ALU.add
                                               ).then_inc(hbo_done, 1)
                            pool.wait_ge(misc_free, add(misc_use(q, c, "QK"), 1))
                            pool.wait_ge(part1_done, nth(b, cc, 1, 1))
                            if has_prior(b, cc, 1):
                                pb, pc = batch(b, cc, -1)
                                pool.wait_ge(spread[pc], add(16 * 2 * NPROD * pb, 16 * 2 * NPROD))
                            pool.tensor_tensor(out=qk_part[:, 2], in0=qk_rest[:], in1=qk_part[:, 1], op=ALU.subtract
                                               ).then_inc(part2_done, 1)
                        if live(b1, c1):
                            pool.wait_ge(norm_done[1], nth(b1, c1, 2, 2))
                            for t in range(ST):
                                pool.tensor_tensor(out=z2g[:, t], in0=z2[:, t], in1=gam_sb[:], op=ALU.mult).then_inc(gam_done, 1)
                            pool.wait_ge(gam_done, nth(b1, c1, 2, 2))
                            if has_prior(b1, c1, 1):
                                pool.wait_ge(norm_done[2], nth(b1, c1, 2, 0))
                            for t in range(ST):
                                pool.tensor_tensor(out=z2b[:, t], in0=z2g[:, t], in1=bet_sb[:], op=ALU.add).then_inc(bet_done, 1)
                            rsqrt(2, b1, c1)
                            pool.wait_ge(norm_done[2], nth(b1, c1, 2, 2))
                            pool.wait_ge(res_loaded[c1 % 2], add(32 * b1, 16 * (c1 // 2) + 16))
                            if has_prior(b1, c1, 2):
                                pool.wait_ge(x1_stored[c1 % 2], add(32 * b1, 16 * (c1 // 2)))
                                pool.wait_ge(norm_done[3], nth(b1, c1, 2, -2))
                            pool.tensor_tensor(out=x1[:, c1 % 2], in0=z3[:], in1=x_res[:, c1 % 2], op=ALU.add
                                               ).then_inc(x1_done, 1)

                    steps(pool, run)

                @block.scalar
                def _(act):
                    for dst, src in ((wg_sb[:], wg.rearrange("e d i -> d e i")), (wu_sb[:], wu.rearrange("e d i -> d e i")),
                                     (wd_sb[:], wd.rearrange("e (t p) d -> p e t d", p=P))):
                        act.dma_start(dst, src).then_inc(w_loaded, 16)

                    def slot(q, c, u):
                        if live(q, c):
                            n = nth(q, c, 8, u)
                            act.wait_ge(st_done, add(n, 1))
                            if u >= 4 or has_prior(q, c, 1):
                                act.wait_ge(av_done, nth(q, c, 8, u - 3))
                            nc.scalar.activation(probs[:, u % 4], ps_st[u % 2][:], ACT.Exp, scale=SCALE).then_inc(exp_done, 1)

                    def run(q, c):
                        b1, c1 = batch(q, c, -1)
                        b2, c2 = batch(q, c, -2)
                        b3, c3 = batch(q, c, 3)
                        slot(q, c, 0)
                        if live(b1, c1):
                            act.wait_ge(av_done, nth(b1, c1, 8, 8))
                            nc.scalar.copy(o_aug[:], ps_av[:]).then_inc(oaug_done, 1)
                        slot(q, c, 1)
                        slot(q, c, 2)
                        if live(b1, c1):
                            act.wait_ge(misc_full, add(misc_use(q, c, "onT"), 1))
                            nc.scalar.copy(onT[:], misc[:, 0:S]).then_inc(misc_free, 1)
                        if live(b3, c3):
                            act.wait_ge(misc_full, add(misc_use(q, c, "hT"), 1))
                            nc.scalar.copy(hT[:], misc[:, 0:S]).then_inc(misc_free, 1)
                        slot(q, c, 3)
                        if live(b3, c3):
                            act.wait_ge(misc_full, add(misc_use(q, c, "QK"), 1))
                            if has_prior(b3, c3, 1):
                                pb, pc = batch(b3, c3, -1)
                                act.wait_ge(spread[pc], add(16 * 2 * NPROD * pb, 16 * 2 * NPROD))
                            else:
                                act.wait_ge(small_loaded, 16 * NSMALL)
                            for n, bias in enumerate((bq_sb, bk_sb)):
                                nc.scalar.activation(qk_part[:, 0, n], misc[:, n * S:(n + 1) * S], ACT.Identity,
                                                     bias=bias[:]).then_inc(part0_done, 1)
                        slot(q, c, 4)
                        if live(b3, c3):
                            act.wait_ge(misc_free, add(misc_use(q, c, "QK"), 1))
                            nc.scalar.copy(qk_part[:, 1], qk_rest[:]).then_inc(part1_done, 1)
                        slot(q, c, 5)
                        slot(q, c, 6)
                        if live(b2, c2):
                            act.wait_ge(misc_full, add(misc_use(q, c, "xnT"), 1))
                            nc.scalar.copy(xnT[:], misc[:, 0:S]).then_inc(misc_free, 1)
                        slot(q, c, 7)
                        if live(b2, c2):
                            act.wait_ge(misc_full, add(misc_use(q, c, "logit"), 1))
                            if isinstance(b2, int):
                                dst = logits[:, :, 4 * b2 + c2:4 * b2 + c2 + 1, :]
                            else:
                                dst = logits[:, :, bass.ds(add(4 * b2, c2), 1), :]
                            nc.scalar.copy(dst, misc[:, 0:ST * E].rearrange("p (t b e) -> p t b e", b=1, e=E)
                                           ).then_inc(misc_free, 1)

                    steps(act, run)

                @block.vector
                def _(dve):
                    dve.memset(qs[:].bitcast(F32), 0.0).then_inc(consts, 1)
                    dve.memset(ks[:].bitcast(F32), 0.0).then_inc(consts, 1)
                    dve.memset(vst[:], 0.0).then_inc(v_done, 1)
                    dve.wait_ge(v_done, 1)
                    dve.wait_ge(consts, 7)
                    dve.memset(ks[MROW:MROW + 3], 1.0).then_inc(consts, 1)
                    vs = vst[:].rearrange("p b t (g s) c -> p (b t g) s c", s=2)
                    dve.memset(vs[:, :, 0, DH:DH + 1], 1.0).then_inc(v_done, 1)
                    dve.memset(vs[:, :, 1, 16 + DH:16 + DH + 1], 1.0).then_inc(v_done, 1)
                    dve.wait_ge(v_done, 3)
                    dve.wait_ge(small_loaded, 16 * NSMALL)

                    def norm_stats(n, b, c, src):
                        if has_prior(b, c, 1):
                            dve.wait_ge(norm_done[n], nth(b, c, 2, 0))
                        for t in range(ST):
                            dve.bn_stats(out=stats[n][:, t], in_=src[:, t]).then_inc(stats_done[n], 1)
                        dve.wait_ge(stats_done[n], nth(b, c, 2, 2))
                        settled(dve)
                        for t in range(ST):
                            dve.bn_aggr(out=mv[n][:, t], in_=stats[n][:, t]).then_inc(mv_done[n], 1)

                    def norm_apply(n, b, c, dst, src):
                        dve.wait_ge(rstd_done[n], nth(b, c, 1, 1))
                        for t in range(ST):
                            dve.tensor_scalar(out=dst[:, t], in0=src[:, t], scalar1=mv[n][:, t, 0:1],
                                              scalar2=rstd[n][:, t:t + 1], op0=ALU.subtract, op1=ALU.mult
                                              ).then_inc(norm_done[n], 1)

                    def slot_max(q, c, k):
                        b, cc = batch(q, c, 1 if k < 8 else 2)
                        if not live(b, cc):
                            return
                        kk = (k + 8) % 16
                        t, hh = kk // 8, kk % 8 * 2
                        dve.wait_ge(s_done, nth(b, cc, 16, kk + 1))
                        dve.tensor_reduce(out=nm[:, cc % 2, t, hh:hh + 2], in_=ps_s[k % 2][:], axis=AX.X, op=ALU.max,
                                          negate=True).then_inc(max_done, 1)

                    def run(q, c):
                        bm, cm = batch(q, c, 1)
                        b1, c1 = batch(q, c, -1)
                        b2, c2 = batch(q, c, -2)
                        b3, c3 = batch(q, c, 3)
                        for k in range(16):
                            slot_max(q, c, k)
                            if k == 0 and live(b3, c3):
                                dve.wait_ge(x_loaded[c3 % 2], add(32 * b3, 16 * (c3 // 2) + 16))
                                norm_stats(0, b3, c3, x_in[:, c3 % 2])
                            if k == 1 and live(b2, c2):
                                dve.wait_ge(x1_done, nth(b2, c2, 1, 1))
                                norm_stats(3, b2, c2, x1[:, c2 % 2])
                            if k == 2 and live(b1, c1):
                                dve.wait_ge(misc_full, add(misc_use(q, c, "OT"), 1))
                                o = misc[:].rearrange("p (h c) -> p h c", c=16)
                                dve.reciprocal(o_rec[:], o[:, :, DH]).then_inc(orec_done, 1)
                                dve.wait_ge(orec_done, nth(b1, c1, 1, 1))
                                dve.tensor_tensor(out=o_norm[:].rearrange("p t (h c) -> p (t h) c", c=DH), in0=o[:, :, 0:DH],
                                                  in1=o_rec[:].rearrange("p (h a) -> p h a", a=1).broadcast_to([P, ST * H, DH]),
                                                  op=ALU.mult).then_inc(misc_free, 1)
                            if k == 3 and live(b3, c3):
                                if has_prior(b3, c3, 2):
                                    dve.wait_ge(hbo_done, nth(b3, c3, 1, -1))
                                norm_apply(0, b3, c3, xn1[:, c3 % 2], x_in[:, c3 % 2])
                            if k == 4 and live(b2, c2):
                                if has_prior(b2, c2, 2):
                                    dve.wait_ge(xn_stored[c2 % 2], add(32 * b2, 16 * (c2 // 2)))
                                norm_apply(3, b2, c2, xn2[:, c2 % 2], x1[:, c2 % 2])
                            if k == 7 and live(b1, c1):
                                dve.wait_ge(misc_full, add(misc_use(q, c, "Wo"), 1))
                                dve.wait_ge(hbo_done, nth(b1, c1, 1, 1))
                                dve.tensor_tensor(out=y[:], in0=misc[:, 0:S].rearrange("p (t d) -> p t d", d=D),
                                                  in1=h_bo[:, c1], op=ALU.add).then_inc(misc_free, 1)
                                dve.wait_ge(misc_free, add(misc_use(q, c, "Wo"), 1))
                                norm_stats(1, b1, c1, y)
                            if k == 9 and live(b3, c3):
                                dve.wait_ge(part0_done, nth(b3, c3, 2, 2))
                                if has_prior(b3, c3, 1):
                                    dve.wait_ge(part2_done, nth(b3, c3, 1, 0))
                                for n, bias in enumerate((bq_sb, bk_sb)):
                                    last = dve.scalar_tensor_tensor(out=qk_rest[:, n], in0=misc[:, n * S:(n + 1) * S],
                                                                    scalar=bias[:], in1=qk_part[:, 0, n], op0=ALU.add,
                                                                    op1=ALU.subtract)
                                    last.then_inc((rest_done, misc_free)[n], 1)
                            if k == 8 and live(bm, cm):
                                v = nm[:, cm % 2]
                                dve.wait_ge(max_done, nth(bm, cm, 16, 16))
                                dve.tensor_copy(nm_part[:, :, 0], v).then_inc(nm0_done, 1)
                                dve.wait_ge(nm0_done, nth(bm, cm, 1, 1))
                                dve.tensor_tensor(out=nm_rest[:], in0=v, in1=nm_part[:, :, 0], op=ALU.subtract).then_inc(nmr_done, 1)
                                dve.wait_ge(nmr_done, nth(bm, cm, 1, 1))
                                dve.tensor_copy(nm_part[:, :, 1], nm_rest[:]).then_inc(nm1_done, 1)
                                dve.wait_ge(nm1_done, nth(bm, cm, 1, 1))
                                dve.tensor_tensor(out=nm_part[:, :, 2], in0=nm_rest[:], in1=nm_part[:, :, 1],
                                                  op=ALU.subtract).then_inc(nm2_done, 1)
                            if k == 10 and live(b1, c1):
                                norm_apply(1, b1, c1, z2, y)
                            if k == 10 and live(b3, c3):
                                dve.wait_ge(misc_full, add(misc_use(q, c, "V"), 1))
                                if has_prior(b3, c3, 4):
                                    dve.wait_ge(av_done, nth(b3, c3, 8, -24))
                                for t in range(ST):
                                    vd = vst[:, c3, t].rearrange("p (g s) c -> p g (s c)", s=2)
                                    src = misc[:, t * D:(t + 1) * D].rearrange("p (g s c) -> p g s c", s=2, c=DH)
                                    bias = bv_sb[:].rearrange("p (g s c) -> p g s c", s=2, c=DH)
                                    for s2 in range(2):
                                        last = dve.tensor_tensor(out=vd[:, :, 48 * s2:48 * s2 + DH], in0=src[:, :, s2],
                                                                 in1=bias[:, :, s2], op=ALU.add)
                                        last.then_inc(misc_free if (t, s2) == (ST - 1, 1) else v_done, 1)
                            if k == 12 and live(bm, cm):
                                dve.wait_ge(misc_full, add(misc_use(q, c, "nmT"), 1))
                                if has_prior(bm, cm, 1):
                                    pb, pc = batch(bm, cm, -1)
                                    dve.wait_ge(nm_spread[pc], add(16 * pb, 16))
                                dve.tensor_copy(nmT[:], misc[0:3 * H, 0:S // 2].bitcast(BF16)).then_inc(misc_free, 1)
                            if k == 13 and live(b1, c1):
                                dve.wait_ge(bet_done, nth(b1, c1, 2, 2))
                                norm_stats(2, b1, c1, z2b)
                            if k == 15 and live(b1, c1):
                                if has_prior(b1, c1, 1):
                                    dve.wait_ge(x1_done, nth(b1, c1, 1, 0))
                                norm_apply(2, b1, c1, z3, z2b)

                    steps(dve, run)

                @block.tensor
                def _(pe):
                    pe.wait_ge(consts, 8)
                    pe.wait_ge(small_loaded, 16 * NSMALL)
                    pe.wait_ge(v_done, 3)

                    def slot_scores(q, c, k):
                        b, cc = batch(q, c, 1 if k < 8 else 2)
                        if not live(b, cc):
                            return
                        kk = (k + 8) % 16
                        t, hh = kk // 8, kk % 8 * 2
                        if kk == 0:
                            pe.wait_ge(spread[cc], add(16 * 2 * NPROD * b, 16 * 2 * NPROD))
                        if kk >= 2 or has_prior(b, cc, 1):
                            pe.wait_ge(max_done, nth(b, cc, 16, kk - 1))
                        for n in range(2):
                            last = nc.tensor.matmul(ps_s[k % 2][:, n], qs[0:MROW, cc, hh + n, t * P:(t + 1) * P],
                                                    ks[0:MROW, cc, hh + n, :], start=True, stop=True)
                        last.then_inc(s_done, 1)

                    def heads(u):
                        j, s2, kt = u // 4, u // 2 % 2, u % 2
                        return j, s2, kt, [8 * j + 2 * g + s2 for g in range(4)]

                    def slot_st(q, c, u):
                        if not live(q, c):
                            return
                        j, s2, kt, hs = heads(u)
                        if u == 0:
                            pe.wait_ge(nm_spread[c], add(16 * q, 16))
                        if u >= 2 or has_prior(q, c, 1):
                            pe.wait_ge(exp_done, nth(q, c, 8, u - 1))
                        for g, hd in enumerate(hs):
                            last = nc.tensor.matmul(ps_st[u % 2][:, g], ks[0:KROWS, c, hd, kt * P:(kt + 1) * P],
                                                    qs[0:KROWS, c, hd, :], start=True, stop=True)
                        last.then_inc(st_done, 1)

                    def slot_av(q, c, u):
                        if not live(q, c):
                            return
                        j, s2, kt, hs = heads(u)
                        pe.wait_ge(exp_done, nth(q, c, 8, u + 1))
                        if u == 0:
                            if has_prior(q, c, 1):
                                pe.wait_ge(oaug_done, nth(q, c, 1, 0))
                        for g, hd in enumerate(hs):
                            last = nc.tensor.matmul(ps_av[32 * g:32 * g + 32, j], vst[:, c, kt, hd], probs[:, u % 4, g],
                                                    start=(s2 == 0 and kt == 0), stop=(s2 == 1 and kt == 1))
                        last.then_inc(av_done, 1)

                    def free(q, c, name):
                        n = misc_use(q, c, name)
                        if not isinstance(n, int) or n > 0:
                            pe.wait_ge(misc_free, n)

                    def run(q, c):
                        bm, cm = batch(q, c, 1)
                        b1, c1 = batch(q, c, -1)
                        b2, c2 = batch(q, c, -2)
                        b3, c3 = batch(q, c, 3)
                        for k in range(16):
                            u = k // 2
                            if k % 2 == 0:
                                slot_st(q, c, u)
                            slot_scores(q, c, k)
                            if k % 2 == 0:
                                if u:
                                    slot_av(q, c, u - 1)
                                else:
                                    slot_av(b1, c1, 7)
                            if k == 2 and live(b1, c1):
                                pe.wait_ge(oaug_done, nth(b1, c1, 1, 1))
                                free(q, c, "OT")
                                for t in range(ST):
                                    for j in range(2):
                                        last = nc.tensor.transpose(misc[:, (2 * t + j) * P:(2 * t + j + 1) * P],
                                                                   o_aug[:, j, t * P:(t + 1) * P], ident[:])
                                last.then_inc(misc_full, 1)
                            if k == 5 and live(b1, c1):
                                free(q, c, "onT")
                                for t in range(ST):
                                    last = nc.tensor.transpose(misc[:, t * P:(t + 1) * P], o_norm[:, t], ident[:])
                                last.then_inc(misc_full, 1)
                            if k == 6 and live(b3, c3):
                                pe.wait_ge(h_done, nth(b3, c3, 1, 1))
                                free(q, c, "hT")
                                for t in range(ST):
                                    last = nc.tensor.transpose(misc[:, t * P:(t + 1) * P], h[:, c3 % 2, t], ident[:])
                                last.then_inc(misc_full, 1)
                            if k == 7 and live(b1, c1):
                                free(q, c, "Wo")
                                for t in range(ST):
                                    last = nc.tensor.matmul(misc[:, t * D:(t + 1) * D], onT[:, t * P:(t + 1) * P], wo_sb[:],
                                                            start=True, stop=True)
                                last.then_inc(misc_full, 1)
                            if k == 8 and live(b3, c3):
                                free(q, c, "QK")
                                for n, w in enumerate((wq_sb, wk_sb)):
                                    last = nc.tensor.matmul(misc[:, n * S:(n + 1) * S], w[:], hT[:], start=True, stop=True)
                                last.then_inc(misc_full, 1)
                            if k == 10 and live(b3, c3):
                                free(q, c, "V")
                                for t in range(ST):
                                    last = nc.tensor.matmul(misc[:, t * D:(t + 1) * D], hT[:, t * P:(t + 1) * P], wv_sb[:],
                                                            start=True, stop=True)
                                last.then_inc(misc_full, 1)
                            if k == 12 and live(bm, cm):
                                pe.wait_ge(nm2_done, nth(bm, cm, 1, 1))
                                free(q, c, "nmT")
                                settled(pe)
                                for t in range(ST):
                                    last = nc.tensor.transpose(misc[0:3 * H, t * P // 2:(t + 1) * P // 2].bitcast(BF16),
                                                               nm_part[:, t].rearrange("p a h -> p (a h)"), identb[:])
                                last.then_inc(misc_full, 1)
                            if k == 13 and live(b2, c2):
                                pe.wait_ge(norm_done[3], nth(b2, c2, 2, 2))
                                free(q, c, "xnT")
                                for t in range(ST):
                                    last = nc.tensor.transpose(misc[:, t * P:(t + 1) * P], xn2[:, c2 % 2, t], ident[:])
                                last.then_inc(misc_full, 1)
                            if k == 15 and live(b2, c2):
                                free(q, c, "logit")
                                for t in range(ST):
                                    last = nc.tensor.matmul(misc[:, t * E:(t + 1) * E], xnT[:, t * P:(t + 1) * P],
                                                            gate_sb[:], start=True, stop=True)
                                last.then_inc(misc_full, 1)

                    steps(pe, run)

        with ExitStack() as rctx:
            def sr(name, shape, dt=F32):
                return sb(name, shape, dt, rctx)

            R = B * E // P
            RB = B // R
            ex = sr("ex", [P, ST * B, E])
            aff = sr("aff", [P, ST, B, E])
            row = sr("row", [P, ST * B])
            rowr = sr("rowr", [P, ST * B])
            scan = sr("scan", [P, R, S])
            top_gate = sr("top_gate", [P, R, 2, CAP])
            top_idx = sr("top_idx", [P, R, CAP], U32)
            top_token = sr("top_token", [P, R, 2, CAP])
            ps_aff = ps("ps_aff", [P, R, S], F32, rctx)
            ps_top = ps("ps_top", [P, R, 2, P], F32, rctx)
            r_dve, r_act, r_aff, r_top = sem("r_dve"), sem("r_act"), sem("r_aff"), sem("r_top")
            CHAIN_AFF = 5
            CHAIN_TOP = 4 + 24 * R

            with nc.Block() as block:
                @block.vector
                def _(dve):
                    chain = [0]

                    def link(ins):
                        chain[0] += 1
                        ins.then_inc(r_dve, 1)
                        dve.wait_ge(r_dve, chain[0])

                    lv = logits[:].rearrange("p t b e -> p (t b) e")
                    wide = lambda v: v[:].rearrange("p (n a) -> p n a", a=1).broadcast_to([P, ST * B, E])
                    link(dve.tensor_reduce(out=row[:], in_=lv, axis=AX.X, op=ALU.max))
                    link(dve.tensor_tensor(out=lv, in0=lv, in1=wide(row), op=ALU.subtract))
                    dve.wait_ge(r_act, 1)
                    link(dve.tensor_reduce(out=row[:], in_=ex[:], axis=AX.X, op=ALU.add))
                    link(dve.reciprocal(rowr[:], row[:]))
                    link(dve.tensor_tensor(out=aff[:].rearrange("p t b e -> p (t b) e"), in0=ex[:], in1=wide(rowr), op=ALU.mult))
                    dve.wait_ge(r_aff, 1)
                    link(dve.tensor_copy(scan[:], ps_aff[:]))
                    for n in range(0, CAP, 8):
                        for r in range(R):
                            link(dve.max(out=top_gate[:, r, 0, n:n + 8], in_=scan[:, r]))
                        for r in range(R):
                            link(dve.max_index(out=top_idx[:, r, n:n + 8], in_max=top_gate[:, r, 0, n:n + 8], in_values=scan[:, r]))
                            link(dve.match_replace(out=scan[:, r], in_to_replace=top_gate[:, r, 0, n:n + 8],
                                                   in_values=scan[:, r], imm_value=-1.0))
                    dve.tensor_copy(top_gate[:, :, 1], top_gate[:, :, 0]).then_inc(r_top, 1)
                    for n in range(2):
                        dve.tensor_copy(top_token[:, :, n], top_idx[:]).then_inc(r_top, 1)
                    dve.wait_ge(r_aff, 2)
                    for n, dst in enumerate((slot_token, slot_gate)):
                        for half in range(2):
                            rows = slice(half * CAP, (half + 1) * CAP)
                            v = ps_top[rows, :, n].rearrange("p r (b m two) -> p r b m two", m=M, two=2)
                            for r in range(R):
                                dve.tensor_copy(dst[rows, r * RB:(r + 1) * RB], v[:, r, :, :, half]).then_inc(r_top, 1)

                @block.scalar
                def _(act):
                    act.wait_ge(r_dve, 2)
                    nc.scalar.activation(ex[:], logits[:].rearrange("p t b e -> p (t b) e"), ACT.Exp).then_inc(r_act, 1)

                @block.tensor
                def _(pe):
                    pe.wait_ge(r_dve, CHAIN_AFF)
                    for r in range(R):
                        for t in range(ST):
                            last = nc.tensor.transpose(ps_aff[:, r, t * P:(t + 1) * P],
                                                       aff[:, t, r * RB:(r + 1) * RB].rearrange("p b e -> p (b e)"), ident[:])
                    last.then_inc(r_aff, 1)
                    pe.wait_ge(r_top, 3)
                    for r in range(R):
                        for n, src in enumerate((top_token, top_gate)):
                            last = nc.tensor.transpose(ps_top[:, r, n], src[:, r].rearrange("p a j -> p (a j)"), ident[:])
                    last.then_inc(r_aff, 1)

        with ExitStack() as ectx:
            def se(name, shape, dt=F32):
                return sb(name, shape, dt, ectx)

            tok = se("tok", [P, GB, M])
            gat = se("gat", [P, GB, M])
            xng = se("xng", [P, GB, ST, D])
            x1g = se("x1g", [P, GB, ST, D])
            iota = se("iota", [P, S])
            pick = se("pick", [P, 2, M, S], BF16)
            pickT = se("pickT", [P, 2, ST, M * P])
            xeT = se("xeT", [P, E, GB * CAP])
            silu = se("silu", [P, 2, GB * CAP])
            hid = se("hid", [P, 2, IT, GB * CAP])
            xe = se("xe", [P, M, GB, D])
            put = se("put", [P, 2, M, S])
            est = se("est", [P, ST, 6])
            emv = se("emv", [P, ST, 2])
            eve = se("eve", [P, ST])
            ers = se("ers", [P, ST])
            zn = se("zn", [P, ST, D])
            res = se("res", [P, 2, ST, D])

            ps_g = [ps(f"ps_g{n}", [P, GB * CAP], F32, ectx) for n in range(2)]
            ps_u = [ps(f"ps_u{n}", [P, GB * CAP], F32, ectx) for n in range(2)]
            ps_d = ps("ps_d", [P, GB, D], F32, ectx)
            ps_pt = ps("ps_pt", [P, ST, M * P], BF16, ectx)
            ps_x = ps("ps_x", [P, E, CAP], F32, ectx)
            ps_f = (ps_pt[:].rearrange("p t n -> p (t n)").bitcast(F32), ps_x[:].rearrange("p e j -> p (e j)"))

            xng_loaded, x1g_loaded = sem("xng_loaded"), sem("x1g_loaded")
            iota_done, tok_done, pick_done, pickT_ps, pickT_done = (sem(n) for n in ("iota_done", "tok_done", "pick_done", "pickT_ps", "pickT_done"))
            x_ps, xeT_done = sem("x_ps"), sem("xeT_done")
            gu_ps, silu_done, hid_done = sem("gu_ps"), sem("silu_done"), sem("hid_done")
            down_ps, xe_done = sem("down_ps"), sem("xe_done")
            put_done, f_ps, est_done, emv_done, eve_done, ers_done, zn_done, res_done = (
                sem(n) for n in ("put_done", "f_ps", "est_done", "emv_done", "eve_done", "ers_done", "zn_done", "res_done"))
            stored = [sem(f"stored{n}") for n in range(2)]
            NU = E * IT

            with nc.Block() as block:
                @block.sync
                def _(sp):
                    for n in range(2):
                        sp.sem_inc(stored[n], 1)
                    with sp.Fori(0, NG) as g:
                        sp.wait_ge(x_ps, GB * g + 1)
                        settled(sp)
                        sp.dma_start(xng[:], xn_dram[bass.ds(GB * g, GB)].rearrange("b p t d -> p b t d")).then_inc(xng_loaded, 16)
                        sp.wait_ge(res_done, GB * g + 1)
                        settled(sp)
                        sp.dma_start(x1g[:], x1_dram[bass.ds(GB * g, GB)].rearrange("b p t d -> p b t d")).then_inc(x1g_loaded, 16)
                        for b in range(GB):
                            sp.wait_ge(res_done, GB * g + (b + 2))
                            settled(sp)
                            sp.dma_start(out[bass.ds(GB * g + b if b else GB * g, 1)].rearrange("b (t p) d -> (b p) t d", p=P),
                                         res[:, b % 2]).then_inc(stored[b % 2], 16)
                    for n in range(2):
                        sp.wait_ge(stored[n], 16 * (B // 2) + 1)

                @block.gpsimd
                def _(pool):
                    pool.iota(iota[:], pattern=[[1, S]], base=0, channel_multiplier=0,
                              allow_small_or_imprecise_dtypes=True).then_inc(iota_done, 1)
                    pool.sem_inc(res_done, 1)
                    with pool.Fori(0, NG) as g:
                        pool.wait_ge(x1g_loaded, 16 * g + 16)
                        for b in range(GB):
                            pool.wait_ge(emv_done, 2 * GB * g + (2 * b + 2))
                            settled(pool)
                            pool.tensor_scalar(out=eve[:], in0=emv[:, :, 1], scalar1=EPS, scalar2=None, op0=ALU.add).then_inc(eve_done, 1)
                            pool.wait_ge(eve_done, GB * g + (b + 1))
                            pool.tensor_tensor(out=ers[:], in0=eve[:], in1=neghalf[:], op=ALU.pow).then_inc(ers_done, 1)
                            pool.wait_ge(zn_done, 2 * GB * g + (2 * b + 3))
                            if b >= 2:
                                pool.wait_ge(stored[b % 2], 16 * (GB // 2) * g + (16 * (b // 2) + 1))
                            else:
                                pool.wait_ge(stored[b % 2], 16 * (GB // 2) * g + 1)
                            pool.tensor_tensor(out=res[:, b % 2], in0=zn[:], in1=x1g[:, b], op=ALU.add).then_inc(res_done, 1)

                @block.scalar
                def _(act):
                    with act.Fori(0, NG) as g:
                        for b in range(GB):
                            act.wait_ge(pickT_ps, GB * g + (b + 1))
                            if b >= 2:
                                act.wait_ge(x_ps, GB * g + b)
                            nc.scalar.copy(pickT[:, b % 2], ps_pt[:]).then_inc(pickT_done, 1)
                        for n in range(NU):
                            act.wait_ge(gu_ps, NU * g + (n + 1))
                            if n >= 2:
                                act.wait_ge(hid_done, NU * g + (n - 1))
                            nc.scalar.activation(silu[:, n % 2], ps_g[n % 2][:], ACT.Silu).then_inc(silu_done, 1)

                def gathered(dve, g, b):
                    dve.wait_ge(x_ps, GB * g + (b + 2))
                    dve.tensor_copy(xeT[:, :, b * CAP:(b + 1) * CAP], ps_x[:]).then_inc(xeT_done, 1)

                def weighted(dve, g, m):
                    dve.wait_ge(down_ps, M * g + (m + 1))
                    dve.tensor_tensor(out=xe[:, m], in0=ps_d[:], in1=gat[:, :, m:m + 1].broadcast_to([P, GB, D]), op=ALU.mult
                                      ).then_inc(xe_done, 1)

                def scatter_rows(dve, g, b):
                    if b >= 2:
                        dve.wait_ge(f_ps, GB * g + (b - 1))
                    for m in range(M):
                        dve.tensor_scalar(out=put[:, b % 2, m], in0=iota[:], scalar1=tok[:, b, m:m + 1],
                                          scalar2=None, op0=ALU.is_equal).then_inc(put_done, 1)

                def last_norm(dve, g, b):
                    dve.wait_ge(f_ps, GB * g + (b + 1))
                    src = ps_f[b % 2]
                    for t in range(ST):
                        dve.bn_stats(out=est[:, t], in_=src[:, t * D:(t + 1) * D]).then_inc(est_done, 1)
                    dve.wait_ge(est_done, 2 * GB * g + (2 * b + 2))
                    settled(dve)
                    for t in range(ST):
                        dve.bn_aggr(out=emv[:, t], in_=est[:, t]).then_inc(emv_done, 1)
                    dve.wait_ge(ers_done, GB * g + (b + 1))
                    if b:
                        dve.wait_ge(res_done, GB * g + (b + 1))
                    else:
                        dve.wait_ge(res_done, GB * g + 1)
                    for t in range(ST):
                        dve.tensor_scalar(out=zn[:, t], in0=src[:, t * D:(t + 1) * D], scalar1=emv[:, t, 0:1],
                                          scalar2=ers[:, t:t + 1], op0=ALU.subtract, op1=ALU.mult).then_inc(zn_done, 1)

                @block.vector
                def _(dve):
                    dve.sem_inc(zn_done, 1)
                    dve.wait_ge(iota_done, 1)
                    with dve.Fori(0, NG) as g:
                        for dst, src in ((tok, slot_token), (gat, slot_gate)):
                            dve.tensor_copy(dst[:], src[:, bass.ds(GB * g, GB)]).then_inc(tok_done, 1)
                        dve.wait_ge(tok_done, 2 * g + 2)
                        for b in range(GB):
                            if b >= 2:
                                dve.wait_ge(pickT_ps, GB * g + (b - 1))
                            for m in range(M):
                                last = dve.tensor_scalar(out=pick[:, b % 2, m], in0=iota[:], scalar1=tok[:, b, m:m + 1],
                                                         scalar2=None, op0=ALU.is_equal)
                                last.then_inc(pick_done, 1)
                            if b >= 1:
                                gathered(dve, g, b - 1)
                            if b == GB - 1:
                                gathered(dve, g, b)
                        for n in range(NU):
                            e, it = n // IT, n % IT
                            dve.wait_ge(silu_done, NU * g + (n + 1))
                            if e >= 2 and it == 0:
                                dve.wait_ge(down_ps, M * g + e // 2)
                            dve.tensor_tensor(out=hid[:, e % 2, it], in0=silu[:, n % 2], in1=ps_u[n % 2][:], op=ALU.mult
                                              ).then_inc(hid_done, 1)
                            if n % (2 * IT) == 3 and n > IT:
                                weighted(dve, g, n // (2 * IT) - 1)
                        weighted(dve, g, M - 1)
                        dve.wait_ge(xe_done, M * g + M)
                        for b in range(GB):
                            scatter_rows(dve, g, b)
                            if b >= 1:
                                last_norm(dve, g, b - 1)
                        last_norm(dve, g, GB - 1)

                @block.tensor
                def _(pe):
                    pe.wait_ge(w_loaded, 48)
                    pe.sem_inc(x_ps, 1)
                    with pe.Fori(0, NG) as g:
                        pe.wait_ge(xng_loaded, 16 * g + 16)
                        pe.wait_ge(zn_done, 2 * GB * g + 1)

                        def transpose_pick(b):
                            pe.wait_ge(pick_done, GB * M * g + M * (b + 1))
                            if b:
                                pe.wait_ge(pickT_done, GB * g + b)
                            for t in range(ST):
                                for m in range(M):
                                    last = nc.tensor.transpose(ps_pt[:, t, m * P:(m + 1) * P],
                                                               pick[:, b % 2, m, t * P:(t + 1) * P], identb[:])
                            last.then_inc(pickT_ps, 1)

                        transpose_pick(0)
                        for b in range(GB):
                            if b + 1 < GB:
                                transpose_pick(b + 1)
                            pe.wait_ge(pickT_done, GB * g + (b + 1))
                            if b:
                                pe.wait_ge(xeT_done, GB * g + b)
                            for t in range(ST):
                                last = nc.tensor.matmul(ps_x[:].rearrange("p e j -> p (e j)"), xng[:, b, t], pickT[:, b % 2, t],
                                                        start=t == 0, stop=t == ST - 1)
                            last.then_inc(x_ps, 1)
                        pe.wait_ge(xeT_done, GB * g + GB)

                        def down(m):
                            pe.wait_ge(hid_done, NU * g + 2 * IT * (m + 1))
                            if m:
                                pe.wait_ge(xe_done, M * g + m)
                            for b in range(GB):
                                for it in range(IT):
                                    for half in range(2):
                                        last = nc.tensor.matmul(ps_d[half * CAP:(half + 1) * CAP, b],
                                                                hid[:, half, it, b * CAP:(b + 1) * CAP],
                                                                wd_sb[:, 2 * m + half, it],
                                                                start=it == 0, stop=it == IT - 1)
                            last.then_inc(down_ps, 1)

                        for n in range(NU):
                            e, it = n // IT, n % IT
                            if n >= 2:
                                pe.wait_ge(hid_done, NU * g + (n - 1))
                            nc.tensor.matmul(ps_g[n % 2][:], wg_sb[:, e, it * P:(it + 1) * P], xeT[:, e], start=True, stop=True)
                            nc.tensor.matmul(ps_u[n % 2][:], wu_sb[:, e, it * P:(it + 1) * P], xeT[:, e], start=True, stop=True
                                             ).then_inc(gu_ps, 1)
                            if n % (2 * IT) == 1 and n > IT:
                                down(n // (2 * IT) - 1)
                        down(M - 1)
                        pe.wait_ge(xe_done, M * g + M)
                        for b in range(GB):
                            pe.wait_ge(put_done, GB * M * g + M * (b + 1))
                            if b >= 2:
                                pe.wait_ge(zn_done, 2 * GB * g + (2 * b - 1))
                            for t in range(ST):
                                for m in range(M):
                                    last = nc.tensor.matmul(ps_f[b % 2][:, t * D:(t + 1) * D], put[:, b % 2, m, t * P:(t + 1) * P],
                                                            xe[:, m, b], start=m == 0, stop=m == M - 1)
                            last.then_inc(f_ps, 1)


def kernel(**inputs):
    import numpy as np
    import concourse.bacc as bacc
    from concourse import mybir as mb
    from concourse.bass_utils import run_bass_kernel_spmd

    a = {n.split("_", 1)[1]: np.asarray(v) for n, v in inputs.items()}

    def by_lane(w):
        return w.reshape(*w.shape[:-1], H, DH).swapaxes(-1, -2).reshape(w.shape)

    pos = np.arange(S, dtype=np.float32)[:, None]
    div = np.exp(np.arange(0, D, 2, dtype=np.float32) * np.float32(-np.log(10000.0) / D))
    pe_tab = np.zeros((S, D), np.float32)
    pe_tab[:, 0::2] = np.sin(pos * div)
    pe_tab[:, 1::2] = np.cos(pos * div)
    arrays = {
        "x": a["attn_x"], "Wq": by_lane(a["attn_Wq"]), "bq": by_lane(a["attn_bq"]), "Wk": by_lane(a["attn_Wk"]),
        "bk": by_lane(a["attn_bk"]), "Wv": a["attn_Wv"], "bv": a["attn_bv"], "Wo": a["attn_Wo"], "bo": a["attn_bo"],
        "gamma": a["attn_gamma"], "beta": a["attn_beta"], "gate": a["ffn_gate_w"].T,
        "wg": a["ffn_w_gate"].transpose(0, 2, 1), "wu": a["ffn_w_up"].transpose(0, 2, 1),
        "wd": a["ffn_w_down"].transpose(0, 2, 1), "pe_tab": pe_tab,
    }
    arrays = {n: np.ascontiguousarray(v) for n, v in arrays.items()}
    nc = bacc.Bacc("TRN2", target_bir_lowering=False, num_devices=1)
    args = [nc.dram_tensor(n, v.shape, mb.dt.from_np(v.dtype), kind="ExternalInput").ap() for n, v in arrays.items()]
    out = nc.dram_tensor("out", (B, S, D), mb.dt.float32, kind="ExternalOutput").ap()
    build(nc, *args, out)
    r = run_bass_kernel_spmd(nc, [arrays], core_ids=[0])
    return r.results[0]["out"]
```

```python
import concourse.bass as bass
from concourse import mybir
from contextlib import ExitStack

B, S, D, H, E, I = 32, 256, 128, 16, 8, 512
DH = D // H
CAP = S // E * 2
P = 128
ST = S // P
IT = I // P
EPS = 1e-5
SCALE = float(DH) ** -0.5

QPART = (0, 0, 1, 1, 0, 2)
KPART = (0, 1, 0, 1, 2, 0)
NPROD = len(QPART)
MROW = NPROD * DH
KROWS = MROW + 3
ONES = 32
PAIR = 1 + 0x3F80 / 2 ** 23

NB4 = 4
LOOP0, NLOOP = 4, 6
FIRST, LAST = -4, B + 2
WARM_STEP, WARM = 0, 10
GB = 8
NG = B // GB
M = E // 2


def add(q, k):
    return q + k if k else q


def live(q, c):
    return not isinstance(q, int) or 0 <= 4 * q + c < B


def has_prior(q, c, n):
    return not isinstance(q, int) or 4 * q + c >= n


def batch(q, c, d):
    return add(q, (c + d) // 4), (c + d) % 4


def nth(q, c, k, m):
    return add(4 * k * q, k * c + m)


MISC = (("xnT", -3), ("logit", -3), ("OT", -1), ("onT", -1), ("Wo", -1), ("hT", 3), ("QK", 3), ("nmT", 1), ("V", 3))


def misc_use(q, c, name):
    if not isinstance(q, int):
        return add(4 * len(MISC) * q, len(MISC) * (c - LOOP0) + misc_use(0, LOOP0, name))
    s, n = 4 * q + c, 0
    for t in range(FIRST, s + 1):
        for use, d in MISC:
            if t == s and use == name:
                return n
            n += 0 <= t + d < B
    raise ValueError(name)


def build(nc, x, Wq, bq, Wk, bk, Wv, bv, Wo, bo, gamma, beta, gate, wg, wu, wd, pe_tab, out):
    F32, F32R, BF16, U32 = mybir.dt.float32, mybir.dt.float32r, mybir.dt.bfloat16, mybir.dt.uint32
    ALU, ACT, AX = mybir.AluOpType, mybir.ActivationFunctionType, mybir.AxisListType
    top = ExitStack()
    names = [0]

    def sem(name):
        return top.enter_context(nc.semaphore(name))

    def steps(eng, run):
        for s in range(FIRST, LOOP0):
            run(s // 4, s % 4)
        with eng.Fori(0, NLOOP) as g:
            for j in range(4):
                run(add(g, (LOOP0 + j) // 4), (LOOP0 + j) % 4)
        for s in range(LOOP0 + 4 * NLOOP, LAST + 1):
            run(s // 4, s % 4)

    with top:
        def sb(name, shape, dt=F32, ctx=top):
            return ctx.enter_context(nc.sbuf_tensor(name, shape, dt))

        def ps(name, shape, dt=F32, ctx=top):
            return ctx.enter_context(nc.psum_tensor(name, shape, dt))

        x1_dram = nc.dram_tensor("x1_scratch", (B, P, ST, D), F32, kind="Internal").ap()
        xn_dram = nc.dram_tensor("xn_scratch", (B, P, ST, D), F32, kind="Internal").ap()

        wg_sb = sb("wg_sb", [P, E, I])
        wu_sb = sb("wu_sb", [P, E, I])
        wd_sb = sb("wd_sb", [P, E, IT, D])
        ident = sb("ident", [P, P])
        identb = sb("identb", [P, P], BF16)
        logits = sb("logits", [P, ST, B, E])
        slot_token = sb("slot_token", [P, B, M])
        slot_gate = sb("slot_gate", [P, B, M])
        neghalf = sb("neghalf", [P, ST])
        w_loaded = sem("w_loaded")
        consts = sem("consts")
        ones_done = sem("ones_done")
        carried = sem("carried")

        def settled(eng):
            eng.sem_inc(carried, 1)


        with ExitStack() as actx:
            def sa(name, shape, dt=F32):
                return sb(name, shape, dt, actx)

            qks = sa("qks", [P, NB4, H, 2, S], BF16)
            qs, ks = qks[:, :, :, 0], qks[:, :, :, 1]
            vst = sa("vst", [P, NB4, ST, H, 32])
            probs = sa("probs", [P, 4, 4, S])
            h_bo = sa("h_bo", [P, NB4, ST, D])
            x_in = sa("x_in", [P, 2, ST, D])
            x_res = sa("x_res", [P, 2, ST, D])
            xn1 = sa("xn1", [P, ST, D])
            h = sa("h", [P, 2, ST, D])
            hT = sa("hT", [P, S])
            qk = sa("qk", [P, 2, S])
            qk_part = sa("qk_part", [P, 6, S], BF16)
            qk_rest = sa("qk_rest", [P, 2, S])
            nm = sa("nm", [P, 2, ST, H])
            nm_part = sa("nm_part", [P, ST, 3, H], BF16)
            nm_rest = sa("nm_rest", [P, ST, H])
            nmT = sa("nmT", [3 * H, S], BF16)
            o_aug = sa("o_aug", [P, 2, S])
            o_rec = sa("o_rec", [P, ST * H])
            o_norm = sa("o_norm", [P, ST, D])
            onT = sa("onT", [P, S])
            y = sa("y", [P, ST, D])
            z2 = sa("z2", [P, ST, D])
            z2g = sa("z2g", [P, ST, D])
            z2b = sa("z2b", [P, ST, D])
            z3 = sa("z3", [P, ST, D])
            x1 = sa("x1", [P, 2, ST, D])
            xn2 = sa("xn2", [P, 2, ST, D])
            xnT = sa("xnT", [P, S])
            stats = [sa(f"stats{n}", [P, ST, 6]) for n in range(4)]
            ks_f32 = ks.bitcast(F32)
            mv = [sa(f"mv{n}", [P, ST, 2]) for n in range(4)]
            veps = [sa(f"veps{n}", [P, ST]) for n in range(4)]
            rstd = [sa(f"rstd{n}", [P, ST]) for n in range(4)]
            negmean = {n: sa(f"negmean{n}", [P, ST]) for n in (0, 3)}
            nmrstd = {n: sa(f"nmrstd{n}", [P, ST]) for n in (0, 3)}
            wq_sb, wk_sb, wv_sb, wo_sb = (sa(n, [P, D]) for n in ("wq_sb", "wk_sb", "wv_sb", "wo_sb"))
            gate_sb = sa("gate_sb", [P, E])
            bq_sb, bk_sb = sa("bq_sb", [P, 1]), sa("bk_sb", [P, 1])
            bo_sb, gam_sb, bet_sb = (sa(n, [P, D]) for n in ("bo_sb", "gam_sb", "bet_sb"))
            pe_sb = sa("pe_sb", [P, ST, D])
            pebo = sa("pebo", [P, ST, D])
            bv_col, bv_wide, bvo = sa("bv_col", [P, 1]), sa("bv_wide", [P, D]), sa("bvo", [P, D])

            ps_s = [ps(f"ps_s{n}", [P, 2, S], F32, actx) for n in range(2)]
            ps_st = [ps(f"ps_st{n}", [P, 4, S], F32, actx) for n in range(2)]
            ps_av = ps("ps_av", [P, 2, S], F32, actx)
            misc = ps("misc", [P, 512], F32, actx)

            small_loaded = sem("small_loaded")
            x_loaded = [sem(f"x_loaded{n}") for n in range(2)]
            res_loaded = [sem(f"res_loaded{n}") for n in range(2)]
            spread = [sem(f"spread{n}") for n in range(NB4)]
            nm_spread = [sem(f"nm_spread{n}") for n in range(NB4)]
            x1_stored = [sem(f"x1_stored{n}") for n in range(2)]
            xn_stored = [sem(f"xn_stored{n}") for n in range(2)]
            misc_full, misc_free = sem("misc_full"), sem("misc_free")
            s_done, max_done = sem("s_done"), sem("max_done")
            st_done, exp_done, av_done = sem("st_done"), sem("exp_done"), sem("av_done")
            oaug_done, orec_done = sem("oaug_done"), sem("orec_done")
            stats_done = [sem(f"stats_done{n}") for n in range(4)]
            mv_done = [sem(f"mv_done{n}") for n in range(4)]
            veps_done = [sem(f"veps_done{n}") for n in range(4)]
            rstd_done = [sem(f"rstd_done{n}") for n in range(4)]
            negmean_done = {n: sem(f"negmean_done{n}") for n in (0, 3)}
            nmrstd_done = {n: sem(f"nmrstd_done{n}") for n in (0, 3)}
            norm_done = [sem(f"norm_done{n}") for n in range(4)]
            h_done, hbo_done = sem("h_done"), sem("hbo_done")
            qk_done, part0_done, rest_done, part1_done, part2_done = (sem(f"qk{n}_done") for n in range(5))
            bvo_done, bvo_ps = sem("bvo_done"), sem("bvo_ps")
            v_done = sem("v_done")
            nm0_done, nmr_done, nm1_done, nm2_done = (sem(f"nm{n}_done") for n in range(4))
            gam_done, bet_done, x1_done = sem("gam_done"), sem("bet_done"), sem("x1_done")
            pebo_done = sem("pebo_done")
            NSMALL = 12

            def x_rows(src, q, c):
                if isinstance(q, int):
                    v = src[4 * q + c:4 * q + c + 1]
                else:
                    v = src[bass.ds(add(4 * q, c), 1)]
                return v.rearrange("b (t p) d -> (b p) t d", p=P)

            def scratch(dst, q, c):
                if isinstance(q, int):
                    v = dst[4 * q + c:4 * q + c + 1]
                else:
                    v = dst[bass.ds(add(4 * q, c), 1)]
                return v.rearrange("b p t d -> (b p) t d")

            with nc.Block() as block:
                @block.sync
                def _(sp):
                    sp.dma_start(x_in[:, 0], x_rows(x, 0, 0)).then_inc(x_loaded[0], 16)
                    for dst, src in ((wq_sb, Wq), (wk_sb, Wk), (wv_sb, Wv), (wo_sb, Wo), (gate_sb, gate)):
                        sp.dma_start(dst[:], src).then_inc(small_loaded, 16)
                    for dst, src in ((bq_sb, bq), (bk_sb, bk), (bv_col, bv)):
                        sp.dma_start(dst[:], src.rearrange("(d a) -> d a", a=1)).then_inc(small_loaded, 16)
                    for dst, src in ((bo_sb, bo), (gam_sb, gamma), (bet_sb, beta)):
                        sp.dma_start(dst[:], src.rearrange("(a d) -> a d", a=1).broadcast_to([P, D])).then_inc(small_loaded, 16)
                    sp.dma_start(pe_sb[:], pe_tab.rearrange("(t p) d -> p t d", p=P)).then_inc(small_loaded, 16)

                    def run(q, c):
                        b4, c4 = batch(q, c, 4)
                        if live(b4, c4) and has_prior(b4, c4, 1):
                            if has_prior(b4, c4, 2):
                                sp.wait_ge(norm_done[0], nth(b4, c4, 2, -2))
                            settled(sp)
                            sp.dma_start(x_in[:, c4 % 2], x_rows(x, b4, c4)).then_inc(x_loaded[c4 % 2], 16)
                        b, cc = batch(q, c, -1)
                        if live(b, cc):
                            if has_prior(b, cc, 2):
                                sp.wait_ge(x1_done, nth(b, cc, 1, -1))
                            settled(sp)
                            sp.dma_start(x_res[:, cc % 2], x_rows(x, b, cc)).then_inc(res_loaded[cc % 2], 16)
                        b, cc = batch(q, c, -2)
                        if live(b, cc):
                            sp.wait_ge(x1_done, nth(b, cc, 1, 1))
                            settled(sp)
                            sp.dma_start(scratch(x1_dram, b, cc), x1[:, cc % 2]).then_inc(x1_stored[cc % 2], 16)
                        b, cc = batch(q, c, 1)
                        if live(b, cc):
                            sp.wait_ge(misc_free, add(misc_use(q, c, "nmT"), 1))
                            sp.dma_start(qs[MROW:MROW + 3, cc], nmT[:]).then_inc(nm_spread[cc], 16)
                        b, cc = batch(q, c, 3)
                        if live(b, cc):
                            if has_prior(b, cc, 4):
                                sp.wait_ge(st_done, nth(b, cc, 8, -24))
                                settled(sp)
                            else:
                                sp.wait_ge(ones_done, NB4)
                            newest = -1
                            for n, (qpart, kpart) in enumerate(zip(QPART, KPART)):
                                if max(qpart, kpart) > newest:
                                    newest = max(qpart, kpart)
                                    sp.wait_ge((part0_done, part1_done, part2_done)[newest], nth(b, cc, 1, 1))
                                    settled(sp)
                                sp.dma_start(qks[n * DH:(n + 1) * DH, cc],
                                             qk_part[:, qpart:4 + kpart:3 + kpart - qpart]).then_inc(spread[cc], 16)
                        b, cc = batch(q, c, -2)
                        if live(b, cc):
                            sp.wait_ge(norm_done[3], nth(b, cc, 2, 2))
                            settled(sp)
                            sp.dma_start(scratch(xn_dram, b, cc), xn2[:, cc % 2]).then_inc(xn_stored[cc % 2], 16)

                    steps(sp, run)
                    for n in range(2):
                        sp.wait_ge(x1_stored[n], 16 * (B // 2))
                        sp.wait_ge(xn_stored[n], 16 * (B // 2))

                @block.gpsimd
                def _(pool):
                    pool.memset(ident[:], 0.0).then_inc(consts, 1)
                    pool.memset(identb[:], 0.0).then_inc(consts, 1)
                    pool.memset(neghalf[:], -0.5).then_inc(consts, 1)
                    pool.wait_ge(consts, 2)
                    for m in (ident, identb):
                        pool.affine_select(out=m[:], in_=m[:], compare_op=ALU.not_equal, fill=1.0, base=0,
                                           pattern=[[-1, P]], channel_multiplier=1).then_inc(consts, 1)
                    pool.memset(vst[:], 0.0).then_inc(v_done, 1)
                    pool.wait_ge(small_loaded, 16 * NSMALL)
                    pool.wait_ge(bvo_done, 2)
                    for t in range(ST):
                        pool.tensor_tensor(out=pebo[:, t], in0=pe_sb[:, t], in1=bvo[:], op=ALU.add).then_inc(pebo_done, 1)
                    pool.wait_ge(pebo_done, ST)

                    def rsqrt(n, b, c):
                        if has_prior(b, c, 1):
                            pool.wait_ge(norm_done[n], nth(b, c, 2, 0))
                        pool.wait_ge(mv_done[n], nth(b, c, 2, 2))
                        settled(pool)
                        pool.tensor_scalar(out=veps[n][:], in0=mv[n][:, :, 1], scalar1=EPS, scalar2=None, op0=ALU.add
                                           ).then_inc(veps_done[n], 1)
                        if n in nmrstd:
                            pool.tensor_scalar(out=negmean[n][:], in0=mv[n][:, :, 0], scalar1=-1.0, scalar2=None, op0=ALU.mult
                                               ).then_inc(negmean_done[n], 1)
                        pool.wait_ge(veps_done[n], nth(b, c, 1, 1))
                        pool.tensor_tensor(out=rstd[n][:], in0=veps[n][:], in1=neghalf[:], op=ALU.pow
                                           ).then_inc(rstd_done[n], 1)
                        if n in nmrstd:
                            pool.wait_ge(negmean_done[n], nth(b, c, 1, 1))
                            pool.wait_ge(rstd_done[n], nth(b, c, 1, 1))
                            pool.tensor_tensor(out=nmrstd[n][:], in0=negmean[n][:], in1=rstd[n][:], op=ALU.mult
                                               ).then_inc(nmrstd_done[n], 1)

                    def run(q, c):
                        b2, c2 = batch(q, c, -2)
                        b3, c3 = batch(q, c, 3)
                        b1, c1 = batch(q, c, -1)
                        bm, cm = batch(q, c, 1)
                        if live(b3, c3):
                            rsqrt(0, b3, c3)
                        if live(b2, c2):
                            rsqrt(2, b2, c2)
                        if live(b3, c3):
                            pool.wait_ge(norm_done[0], nth(b3, c3, 2, 2))
                            if has_prior(b3, c3, 2):
                                pool.wait_ge(qk_done, nth(b3, c3, 1, -1))
                            pool.tensor_tensor(out=h[:, c3 % 2], in0=xn1[:], in1=pe_sb[:], op=ALU.add
                                               ).then_inc(h_done, 1)
                        if live(b2, c2):
                            pool.wait_ge(norm_done[2], nth(b2, c2, 2, 2))
                            pool.wait_ge(res_loaded[c2 % 2], add(32 * b2, 16 * (c2 // 2) + 16))
                            if has_prior(b2, c2, 2):
                                pool.wait_ge(x1_stored[c2 % 2], add(32 * b2, 16 * (c2 // 2)))
                                pool.wait_ge(norm_done[3], nth(b2, c2, 2, -2))
                            pool.tensor_tensor(out=x1[:, c2 % 2], in0=z3[:], in1=x_res[:, c2 % 2], op=ALU.add
                                               ).then_inc(x1_done, 1)
                        if live(bm, cm):
                            v = nm[:, cm % 2]
                            pool.wait_ge(max_done, nth(bm, cm, 16, 16))
                            if has_prior(bm, cm, 1):
                                pbm, pcm = batch(bm, cm, -1)
                                pool.wait_ge(nm_spread[pcm], add(16 * pbm, 16))
                            settled(pool)
                            pool.tensor_copy(nm_part[:, :, 0], v).then_inc(nm0_done, 1)
                            pool.wait_ge(nm0_done, nth(bm, cm, 1, 1))
                            pool.tensor_tensor(out=nm_rest[:], in0=v, in1=nm_part[:, :, 0], op=ALU.subtract).then_inc(nmr_done, 1)
                            pool.wait_ge(nmr_done, nth(bm, cm, 1, 1))
                            settled(pool)
                            pool.tensor_copy(nm_part[:, :, 1], nm_rest[:]).then_inc(nm1_done, 1)
                            pool.wait_ge(nm1_done, nth(bm, cm, 1, 1))
                            pool.tensor_tensor(out=nm_part[:, :, 2], in0=nm_rest[:], in1=nm_part[:, :, 1],
                                               op=ALU.subtract).then_inc(nm2_done, 1)
                        if live(b2, c2):
                            rsqrt(3, b2, c2)
                        if live(b3, c3):
                            if has_prior(b3, c3, 4):
                                pool.wait_ge(misc_free, add(misc_use(q, c, "Wo"), 1))
                            pool.tensor_tensor(out=h_bo[:, c3], in0=xn1[:], in1=pebo[:], op=ALU.add
                                               ).then_inc(hbo_done, 1)
                        if live(b1, c1):
                            rsqrt(1, b1, c1)
                        if live(b3, c3):
                            pool.wait_ge(part0_done, nth(b3, c3, 1, 1))
                            pool.tensor_tensor(out=qk_rest[:], in0=qk[:], in1=qk_part[:, 0::3], op=ALU.subtract
                                               ).then_inc(rest_done, 1)
                        if live(b1, c1):
                            pool.wait_ge(norm_done[1], nth(b1, c1, 2, 2))
                            for t in range(ST):
                                pool.tensor_tensor(out=z2g[:, t], in0=z2[:, t], in1=gam_sb[:], op=ALU.mult).then_inc(gam_done, 1)
                            pool.wait_ge(gam_done, nth(b1, c1, 2, 2))
                            if has_prior(b1, c1, 1):
                                pool.wait_ge(norm_done[2], nth(b1, c1, 2, 0))
                            for t in range(ST):
                                pool.tensor_tensor(out=z2b[:, t], in0=z2g[:, t], in1=bet_sb[:], op=ALU.add).then_inc(bet_done, 1)
                        if live(b3, c3):
                            pool.wait_ge(part1_done, nth(b3, c3, 1, 1))
                            pool.tensor_tensor(out=qk_part[:, 2::3], in0=qk_rest[:], in1=qk_part[:, 1::3], op=ALU.subtract
                                               ).then_inc(part2_done, 1)

                    steps(pool, run)

                @block.scalar
                def _(act):
                    for dst, src in ((wg_sb[:], wg.rearrange("e d i -> d e i")), (wu_sb[:], wu.rearrange("e d i -> d e i")),
                                     (wd_sb[:], wd.rearrange("e (t p) d -> p e t d", p=P))):
                        act.dma_start(dst, src).then_inc(w_loaded, 16)

                    def slot(q, c, u):
                        if live(q, c):
                            n = nth(q, c, 8, u)
                            act.wait_ge(st_done, add(n, 1))
                            if u >= 4 or has_prior(q, c, 1):
                                act.wait_ge(av_done, nth(q, c, 8, u - 3))
                            nc.scalar.activation(probs[:, u % 4], ps_st[u % 2][:], ACT.Exp, scale=SCALE).then_inc(exp_done, 1)

                    def norm_apply(n, b, c, dst, src):
                        act.wait_ge(nmrstd_done[n], nth(b, c, 1, 1))
                        for t in range(ST):
                            nc.scalar.activation(dst[:, t], src[:, t], ACT.Identity, bias=nmrstd[n][:, t:t + 1],
                                                 scale=rstd[n][:, t:t + 1]).then_inc(norm_done[n], 1)

                    def run(q, c):
                        b1, c1 = batch(q, c, -1)
                        b2, c2 = batch(q, c, -2)
                        b3, c3 = batch(q, c, 3)
                        br, cr = batch(q, c, -3)
                        if live(br, cr):
                            act.wait_ge(misc_full, add(misc_use(q, c, "xnT"), 1))
                            nc.scalar.copy(xnT[:], misc[:, 0:S]).then_inc(misc_free, 1)
                        slot(q, c, 0)
                        if live(b1, c1):
                            act.wait_ge(av_done, nth(b1, c1, 8, 8))
                            nc.scalar.copy(o_aug[:], ps_av[:]).then_inc(oaug_done, 1)
                        if live(br, cr):
                            act.wait_ge(misc_full, add(misc_use(q, c, "logit"), 1))
                            if isinstance(br, int):
                                dst = logits[:, :, 4 * br + cr:4 * br + cr + 1, :]
                            else:
                                dst = logits[:, :, bass.ds(add(4 * br, cr), 1), :]
                            nc.scalar.copy(dst, misc[:, 0:ST * E].rearrange("p (t b e) -> p t b e", b=1, e=E)
                                           ).then_inc(misc_free, 1)
                        slot(q, c, 1)
                        if live(b3, c3):
                            if has_prior(b3, c3, 1):
                                act.wait_ge(hbo_done, nth(b3, c3, 1, 0))
                            norm_apply(0, b3, c3, xn1, x_in[:, c3 % 2])
                        slot(q, c, 2)
                        if live(b1, c1):
                            act.wait_ge(misc_full, add(misc_use(q, c, "onT"), 1))
                            nc.scalar.copy(onT[:], misc[:, 0:S]).then_inc(misc_free, 1)
                        slot(q, c, 3)
                        slot(q, c, 4)
                        if live(b3, c3):
                            act.wait_ge(misc_full, add(misc_use(q, c, "hT"), 1))
                            nc.scalar.copy(hT[:], misc[:, 0:S]).then_inc(misc_free, 1)
                        slot(q, c, 5)
                        if live(b3, c3):
                            act.wait_ge(misc_full, add(misc_use(q, c, "QK"), 1))
                            if has_prior(b3, c3, 1):
                                pb, pc = batch(b3, c3, -1)
                                act.wait_ge(spread[pc], add(16 * NPROD * pb, 16 * NPROD))
                            else:
                                act.wait_ge(small_loaded, 16 * NSMALL)
                            for n, bias in enumerate((bq_sb, bk_sb)):
                                nc.scalar.activation(qk[:, n], misc[:, n * S:(n + 1) * S], ACT.Identity,
                                                     bias=bias[:]).then_inc((qk_done, misc_free)[n], 1)
                            act.wait_ge(misc_free, add(misc_use(q, c, "QK"), 1))
                            act.wait_ge(qk_done, nth(b3, c3, 1, 1))
                            nc.scalar.copy(qk_part[:, 0::3], qk[:]).then_inc(part0_done, 1)
                        slot(q, c, 6)
                        if live(b2, c2):
                            if has_prior(b2, c2, 2):
                                act.wait_ge(xn_stored[c2 % 2], add(32 * b2, 16 * (c2 // 2)))
                            norm_apply(3, b2, c2, xn2[:, c2 % 2], x1[:, c2 % 2])
                        if live(b3, c3):
                            act.wait_ge(misc_full, add(misc_use(q, c, "V"), 1))
                            if has_prior(b3, c3, 4):
                                act.wait_ge(av_done, nth(b3, c3, 8, -24))
                            else:
                                act.wait_ge(v_done, 3)
                            vd = vst[:, c3].rearrange("p t (g s) c -> p t g (s c)", s=2)
                            src = misc[:, 0:S].rearrange("p (t g s c) -> p t g s c", t=ST, s=2, c=DH)
                            for s2 in range(2):
                                nc.scalar.copy(vd[:, :, :, 48 * s2:48 * s2 + DH], src[:, :, :, s2]).then_inc((v_done, misc_free)[s2], 1)
                        slot(q, c, 7)
                        if live(b3, c3):
                            act.wait_ge(rest_done, nth(b3, c3, 1, 1))
                            nc.scalar.copy(qk_part[:, 1::3], qk_rest[:]).then_inc(part1_done, 1)

                    steps(act, run)

                @block.vector
                def _(dve):
                    for n in range(NB4):
                        dve.memset(ks_f32[ONES:KROWS, n], PAIR).then_inc(ones_done, 1)
                    dve.wait_ge(v_done, 1)
                    vs = vst[:].rearrange("p b t (g s) c -> p (b t g) s c", s=2)
                    dve.memset(vs[:, :, 0, DH:DH + 1], 1.0).then_inc(v_done, 1)
                    dve.memset(vs[:, :, 1, 16 + DH:16 + DH + 1], 1.0).then_inc(v_done, 1)
                    dve.wait_ge(v_done, 3)
                    dve.wait_ge(small_loaded, 16 * NSMALL)
                    dve.tensor_copy(bv_wide[:], bv_col[:].broadcast_to([P, D])).then_inc(bvo_done, 1)
                    dve.wait_ge(bvo_ps, 1)
                    dve.tensor_tensor(out=bvo[:], in0=misc[:, 0:D], in1=bo_sb[:], op=ALU.add).then_inc(bvo_done, 1)

                    heads16 = misc[:].rearrange("p (h c) -> p h c", c=16)

                    def norm_stats(n, b, c, src):
                        if has_prior(b, c, 1):
                            dve.wait_ge(mv_done[n], nth(b, c, 2, 0))
                        for t in range(ST):
                            dve.bn_stats(out=stats[n][:, t], in_=src[:, t]).then_inc(stats_done[n], 1)

                    def norm_aggr(n, b, c):
                        if has_prior(b, c, 1):
                            dve.wait_ge(norm_done[n], nth(b, c, 2, 0))
                        dve.wait_ge(stats_done[n], nth(b, c, 2, 2))
                        settled(dve)
                        for t in range(ST):
                            dve.bn_aggr(out=mv[n][:, t], in_=stats[n][:, t]).then_inc(mv_done[n], 1)

                    def norm_apply(n, b, c, dst, src):
                        dve.wait_ge(rstd_done[n], nth(b, c, 1, 1))
                        for t in range(ST):
                            dve.tensor_scalar(out=dst[:, t], in0=src[:, t], scalar1=mv[n][:, t, 0:1],
                                              scalar2=rstd[n][:, t:t + 1], op0=ALU.subtract, op1=ALU.mult
                                              ).then_inc(norm_done[n], 1)

                    def slot_max(q, c, k):
                        b, cc = batch(q, c, 1 if k < 8 else 2)
                        if not live(b, cc):
                            return
                        kk = (k + 8) % 16
                        t, hh = kk // 8, kk % 8 * 2
                        dve.wait_ge(s_done, nth(b, cc, 16, kk + 1))
                        dve.tensor_reduce(out=nm[:, cc % 2, t, hh:hh + 2], in_=ps_s[k % 2][:], axis=AX.X, op=ALU.max,
                                          negate=True).then_inc(max_done, 1)

                    def run(q, c):
                        bm, cm = batch(q, c, 1)
                        b1, c1 = batch(q, c, -1)
                        b2, c2 = batch(q, c, -2)
                        b3, c3 = batch(q, c, 3)
                        b4, c4 = batch(q, c, 4)
                        for k in range(16):
                            if k == 12 and live(bm, cm):
                                dve.wait_ge(misc_full, add(misc_use(q, c, "nmT"), 1))
                                if has_prior(bm, cm, 1):
                                    pb, pc = batch(bm, cm, -1)
                                    dve.wait_ge(nm_spread[pc], add(16 * pb, 16))
                                dve.tensor_copy(nmT[:], misc[0:3 * H, 0:S // 2].bitcast(BF16)).then_inc(misc_free, 1)
                            if k == 7 and live(b1, c1):
                                dve.wait_ge(misc_full, add(misc_use(q, c, "Wo"), 1))
                                dve.wait_ge(hbo_done, nth(b1, c1, 1, 1))
                                dve.tensor_tensor(out=y[:], in0=misc[:, 0:S].rearrange("p (t d) -> p t d", d=D),
                                                  in1=h_bo[:, c1], op=ALU.add).then_inc(misc_free, 1)
                            slot_max(q, c, k)
                            if k == 0 and live(b2, c2):
                                dve.wait_ge(bet_done, nth(b2, c2, 2, 2))
                                norm_stats(2, b2, c2, z2b)
                            if k == 1 and live(b2, c2):
                                norm_aggr(2, b2, c2)
                            if k == 3 and live(b1, c1):
                                dve.wait_ge(misc_full, add(misc_use(q, c, "OT"), 1))
                                dve.reciprocal(o_rec[:], heads16[:, :, DH]).then_inc(orec_done, 1)
                                dve.wait_ge(orec_done, nth(b1, c1, 1, 1))
                                dve.tensor_tensor(out=o_norm[:].rearrange("p t (h c) -> p (t h) c", c=DH), in0=heads16[:, :, 0:DH],
                                                  in1=o_rec[:].rearrange("p (h a) -> p h a", a=1).broadcast_to([P, ST * H, DH]),
                                                  op=ALU.mult).then_inc(misc_free, 1)
                            if k == 4 and live(b2, c2):
                                if has_prior(b2, c2, 1):
                                    dve.wait_ge(x1_done, nth(b2, c2, 1, 0))
                                norm_apply(2, b2, c2, z3, z2b)
                            if k == 6 and live(b2, c2):
                                dve.wait_ge(x1_done, nth(b2, c2, 1, 1))
                                norm_stats(3, b2, c2, x1[:, c2 % 2])
                            if k == 7 and live(b2, c2):
                                norm_aggr(3, b2, c2)
                            if k == 8 and live(b1, c1):
                                dve.wait_ge(misc_free, add(misc_use(q, c, "Wo"), 1))
                                norm_stats(1, b1, c1, y)
                            if k == 9 and live(b1, c1):
                                norm_aggr(1, b1, c1)
                            if k == 12 and live(b1, c1):
                                norm_apply(1, b1, c1, z2, y)
                            if k == 14 and live(b4, c4):
                                dve.wait_ge(x_loaded[c4 % 2], add(32 * b4, 16 * (c4 // 2) + 16))
                                norm_stats(0, b4, c4, x_in[:, c4 % 2])
                            if k == 15 and live(b4, c4):
                                norm_aggr(0, b4, c4)

                    steps(dve, run)

                @block.tensor
                def _(pe):
                    pe.wait_ge(consts, 5)
                    pe.wait_ge(small_loaded, 16 * NSMALL)
                    pe.wait_ge(bvo_done, 1)
                    nc.tensor.matmul(misc[:, 0:D], bv_wide[:], wo_sb[:], start=True, stop=True).then_inc(bvo_ps, 1)
                    pe.wait_ge(bvo_done, 2)

                    def slot_scores(q, c, k):
                        b, cc = batch(q, c, 1 if k < 8 else 2)
                        if not live(b, cc):
                            return
                        kk = (k + 8) % 16
                        t, hh = kk // 8, kk % 8 * 2
                        if kk == 0:
                            pe.wait_ge(spread[cc], add(16 * NPROD * b, 16 * NPROD))
                        if kk >= 2 or has_prior(b, cc, 1):
                            pe.wait_ge(max_done, nth(b, cc, 16, kk - 1))
                        for n in range(2):
                            last = nc.tensor.matmul(ps_s[k % 2][:, n], qs[0:MROW, cc, hh + n, t * P:(t + 1) * P],
                                                    ks[0:MROW, cc, hh + n, :], start=True, stop=True)
                        last.then_inc(s_done, 1)

                    def heads(u):
                        j, s2, kt = u // 4, u // 2 % 2, u % 2
                        return j, s2, kt, [8 * j + 2 * g + s2 for g in range(4)]

                    def slot_st(q, c, u):
                        if not live(q, c):
                            return
                        j, s2, kt, hs = heads(u)
                        if u == 0:
                            pe.wait_ge(nm_spread[c], add(16 * q, 16))
                        if u >= 2 or has_prior(q, c, 1):
                            pe.wait_ge(exp_done, nth(q, c, 8, u - 1))
                        for g, hd in enumerate(hs):
                            last = nc.tensor.matmul(ps_st[u % 2][:, g], ks[0:KROWS, c, hd, kt * P:(kt + 1) * P],
                                                    qs[0:KROWS, c, hd, :], start=True, stop=True)
                        last.then_inc(st_done, 1)

                    def slot_av(q, c, u):
                        if not live(q, c):
                            return
                        j, s2, kt, hs = heads(u)
                        pe.wait_ge(exp_done, nth(q, c, 8, u + 1))
                        if u == 0:
                            if has_prior(q, c, 1):
                                pe.wait_ge(oaug_done, nth(q, c, 1, 0))
                        for g, hd in enumerate(hs):
                            last = nc.tensor.matmul(ps_av[32 * g:32 * g + 32, j], vst[:, c, kt, hd], probs[:, u % 4, g],
                                                    start=(s2 == 0 and kt == 0), stop=(s2 == 1 and kt == 1))
                        last.then_inc(av_done, 1)

                    def free(q, c, name):
                        n = misc_use(q, c, name)
                        if not isinstance(n, int) or n > 0:
                            pe.wait_ge(misc_free, n)

                    def run(q, c):
                        bm, cm = batch(q, c, 1)
                        b1, c1 = batch(q, c, -1)
                        b2, c2 = batch(q, c, -2)
                        b3, c3 = batch(q, c, 3)
                        br, cr = batch(q, c, -3)
                        if isinstance(q, int) and 4 * q + c == WARM_STEP:
                            free(q, c, "OT")
                            for n in range(WARM):
                                nc.tensor.matmul(misc[:, 0:P], ident[:], ident[:], start=True, stop=True)
                        if live(br, cr):
                            pe.wait_ge(norm_done[3], nth(br, cr, 2, 2))
                            free(q, c, "xnT")
                            for t in range(ST):
                                last = nc.tensor.transpose(misc[:, t * P:(t + 1) * P], xn2[:, cr % 2, t], ident[:])
                            last.then_inc(misc_full, 1)
                        for k in range(16):
                            u = k // 2
                            if k % 2 == 0:
                                slot_st(q, c, u)
                            if k == 12 and live(bm, cm):
                                pe.wait_ge(nm2_done, nth(bm, cm, 1, 1))
                                free(q, c, "nmT")
                                settled(pe)
                                for t in range(ST):
                                    last = nc.tensor.transpose(misc[0:3 * H, t * P // 2:(t + 1) * P // 2].bitcast(BF16),
                                                               nm_part[:, t].rearrange("p a h -> p (a h)"), identb[:])
                                last.then_inc(misc_full, 1)
                            slot_scores(q, c, k)
                            if k % 2 == 0:
                                if u:
                                    slot_av(q, c, u - 1)
                                else:
                                    slot_av(b1, c1, 7)
                            if k == 1 and live(br, cr):
                                free(q, c, "logit")
                                for t in range(ST):
                                    last = nc.tensor.matmul(misc[:, t * E:(t + 1) * E], xnT[:, t * P:(t + 1) * P],
                                                            gate_sb[:], start=True, stop=True)
                                last.then_inc(misc_full, 1)
                            if k == 2 and live(b1, c1):
                                pe.wait_ge(oaug_done, nth(b1, c1, 1, 1))
                                free(q, c, "OT")
                                for t in range(ST):
                                    for j in range(2):
                                        last = nc.tensor.transpose(misc[:, (2 * t + j) * P:(2 * t + j + 1) * P],
                                                                   o_aug[:, j, t * P:(t + 1) * P], ident[:])
                                last.then_inc(misc_full, 1)
                            if k == 5 and live(b1, c1):
                                free(q, c, "onT")
                                for t in range(ST):
                                    last = nc.tensor.transpose(misc[:, t * P:(t + 1) * P], o_norm[:, t], ident[:])
                                last.then_inc(misc_full, 1)
                            if k == 6 and live(b1, c1):
                                free(q, c, "Wo")
                                for t in range(ST):
                                    last = nc.tensor.matmul(misc[:, t * D:(t + 1) * D], onT[:, t * P:(t + 1) * P], wo_sb[:],
                                                            start=True, stop=True)
                                last.then_inc(misc_full, 1)
                            if k == 8 and live(b3, c3):
                                pe.wait_ge(h_done, nth(b3, c3, 1, 1))
                                free(q, c, "hT")
                                for t in range(ST):
                                    last = nc.tensor.transpose(misc[:, t * P:(t + 1) * P], h[:, c3 % 2, t], ident[:])
                                last.then_inc(misc_full, 1)
                            if k == 10 and live(b3, c3):
                                free(q, c, "QK")
                                for n, w in enumerate((wq_sb, wk_sb)):
                                    last = nc.tensor.matmul(misc[:, n * S:(n + 1) * S], w[:], hT[:], start=True, stop=True)
                                last.then_inc(misc_full, 1)
                            if k == 13 and live(b3, c3):
                                free(q, c, "V")
                                for t in range(ST):
                                    last = nc.tensor.matmul(misc[:, t * D:(t + 1) * D], hT[:, t * P:(t + 1) * P], wv_sb[:],
                                                            start=True, stop=True)
                                last.then_inc(misc_full, 1)

                    steps(pe, run)

        w_hi = [sb(f"w_hi{n}", [P, E, I], F32R) for n in range(2)]
        w_lo = [sb(f"w_lo{n}", [P, E, I], F32R) for n in range(2)]

        with ExitStack() as rctx:
            def sr(name, shape, dt=F32):
                return sb(name, shape, dt, rctx)

            R = B * E // P
            RB = B // R
            ex = sr("ex", [P, ST * B, E])
            aff = sr("aff", [P, ST, B, E])
            row = sr("row", [P, ST * B])
            rowr = sr("rowr", [P, ST * B])
            scan = sr("scan", [P, R, S])
            top_gate = sr("top_gate", [P, R, 2, CAP])
            top_idx = sr("top_idx", [P, R, CAP], U32)
            top_token = sr("top_token", [P, R, 2, CAP])
            ps_aff = ps("ps_aff", [P, R, S], F32, rctx)
            ps_top = ps("ps_top", [P, R, 2, P], F32, rctx)
            r_dve, r_act, r_aff, r_top = sem("r_dve"), sem("r_act"), sem("r_aff"), sem("r_top")
            wh_done, wl_done = sem("wh_done"), sem("wl_done")
            CHAIN_AFF = 5
            CHAIN_TOP = 4 + 24 * R

            with nc.Block() as block:
                @block.vector
                def _(dve):
                    chain = [0]

                    def link(ins):
                        chain[0] += 1
                        ins.then_inc(r_dve, 1)
                        dve.wait_ge(r_dve, chain[0])

                    lv = logits[:].rearrange("p t b e -> p (t b) e")
                    wide = lambda v: v[:].rearrange("p (n a) -> p n a", a=1).broadcast_to([P, ST * B, E])
                    link(dve.tensor_reduce(out=row[:], in_=lv, axis=AX.X, op=ALU.max))
                    link(dve.tensor_tensor(out=lv, in0=lv, in1=wide(row), op=ALU.subtract))
                    dve.wait_ge(r_act, 1)
                    link(dve.tensor_reduce(out=row[:], in_=ex[:], axis=AX.X, op=ALU.add))
                    link(dve.reciprocal(rowr[:], row[:]))
                    link(dve.tensor_tensor(out=aff[:].rearrange("p t b e -> p (t b) e"), in0=ex[:], in1=wide(rowr), op=ALU.mult))
                    dve.wait_ge(r_aff, 1)
                    link(dve.tensor_copy(scan[:], ps_aff[:]))
                    for n in range(0, CAP, 8):
                        for r in range(R):
                            link(dve.max(out=top_gate[:, r, 0, n:n + 8], in_=scan[:, r]))
                        for r in range(R):
                            link(dve.max_index(out=top_idx[:, r, n:n + 8], in_max=top_gate[:, r, 0, n:n + 8], in_values=scan[:, r]))
                            link(dve.match_replace(out=scan[:, r], in_to_replace=top_gate[:, r, 0, n:n + 8],
                                                   in_values=scan[:, r], imm_value=-1.0))
                    dve.tensor_copy(top_gate[:, :, 1], top_gate[:, :, 0]).then_inc(r_top, 1)
                    for n in range(2):
                        dve.tensor_copy(top_token[:, :, n], top_idx[:]).then_inc(r_top, 1)
                    dve.wait_ge(r_aff, 2)
                    for n, dst in enumerate((slot_token, slot_gate)):
                        for half in range(2):
                            rows = slice(half * CAP, (half + 1) * CAP)
                            v = ps_top[rows, :, n].rearrange("p r (b m two) -> p r b m two", m=M, two=2)
                            for r in range(R):
                                dve.tensor_copy(dst[rows, r * RB:(r + 1) * RB], v[:, r, :, :, half]).then_inc(r_top, 1)

                @block.scalar
                def _(act):
                    act.wait_ge(r_dve, 2)
                    nc.scalar.activation(ex[:], logits[:].rearrange("p t b e -> p (t b) e"), ACT.Exp).then_inc(r_act, 1)
                    act.wait_ge(w_loaded, 48)
                    for e in range(0, E, 2):
                        for hi, w in zip(w_hi, (wg_sb, wu_sb)):
                            nc.scalar.copy(hi[:, e:e + 2], w[:, e:e + 2]).then_inc(wh_done, 1)

                @block.gpsimd
                def _(pool):
                    for e in range(0, E, 2):
                        for n, (lo, hi, w) in enumerate(zip(w_lo, w_hi, (wg_sb, wu_sb))):
                            pool.wait_ge(wh_done, e + n + 1)
                            pool.tensor_tensor(out=lo[:, e:e + 2], in0=w[:, e:e + 2], in1=hi[:, e:e + 2], op=ALU.subtract
                                               ).then_inc(wl_done, 1)
                    pool.wait_ge(wl_done, E)

                @block.tensor
                def _(pe):
                    pe.wait_ge(r_dve, CHAIN_AFF)
                    for r in range(R):
                        for t in range(ST):
                            last = nc.tensor.transpose(ps_aff[:, r, t * P:(t + 1) * P],
                                                       aff[:, t, r * RB:(r + 1) * RB].rearrange("p b e -> p (b e)"), ident[:])
                    last.then_inc(r_aff, 1)
                    pe.wait_ge(r_top, 3)
                    for r in range(R):
                        for n, src in enumerate((top_token, top_gate)):
                            last = nc.tensor.transpose(ps_top[:, r, n], src[:, r].rearrange("p a j -> p (a j)"), ident[:])
                    last.then_inc(r_aff, 1)

        with ExitStack() as ectx:
            def se(name, shape, dt=F32):
                return sb(name, shape, dt, ectx)

            NBX = 4
            NU = E * IT
            tok_pick = se("tok_pick", [P, GB, M])
            tok_put = se("tok_put", [P, GB, M])
            gat = se("gat", [P, GB, M])
            xn_rows = se("xn_rows", [P, NBX, ST, D])
            xn_hi = se("xn_hi", [P, 2, ST, D], F32R)
            xn_lo = se("xn_lo", [P, 2, ST, D], F32R)
            x1_rows = se("x1_rows", [P, NBX, ST, D])
            iota = se("iota", [P, S])
            pick = se("pick", [P, 2, M, S], BF16)
            pickT = se("pickT", [P, 2, ST, M * P], F32R)
            xeT_hi = se("xeT_hi", [P, E, GB * CAP], F32R)
            xeT_lo = se("xeT_lo", [P, E, GB * CAP], F32R)
            silu = se("silu", [P, 2, GB * CAP])
            NBH = 3
            hid = se("hid", [P, NBH, IT, GB * CAP])
            put = wg_sb[:].rearrange("p e i -> p (e i)").rearrange("p (b m s) -> p b m s", b=NBX, m=M)
            xe = wu_sb[:].rearrange("p e i -> p (e i)").rearrange("p (m b d) -> p m b d", m=M, b=GB)
            est = se("est", [P, 2, ST, 6])
            emv = se("emv", [P, 2, ST, 2])
            eve = se("eve", [P, ST])
            negm = se("negm", [P, ST])
            ers = se("ers", [P, 2, ST])
            nmr = se("nmr", [P, 2, ST])
            zn = se("zn", [P, 2, ST, D])
            res = se("res", [P, 2, ST, D])

            ps_g = [ps(f"ps_g{n}", [P, GB * CAP], F32, ectx) for n in range(2)]
            ps_u = [ps(f"ps_u{n}", [P, GB * CAP], F32, ectx) for n in range(2)]
            ps_d = ps("ps_d", [P, GB, D], F32, ectx)
            ps_p = ps("ps_p", [P, ST, M * P], BF16, ectx)
            ps_x = ps("ps_x", [P, ST, D], F32, ectx)
            ps_pt = (ps_p[:], ps_d[:, GB // 2:].rearrange("p b d -> p (b d)").bitcast(BF16).rearrange("p (t n) -> p t n", t=ST))
            ps_f = (ps_x[:], ps_d[:, 0:ST])
            ps_fl = ps_f + tuple(t[:].rearrange("p (t d) -> p t d", t=GB // 2)[:, 0:ST] for t in (ps_g[0], ps_u[0]))

            def sum_bank(b, follows):
                return ps_f[b % 2] if follows else ps_fl[b % 4]

            xn_loaded = [sem(f"xn_loaded{n}") for n in range(NBX)]
            x1_loaded = [sem(f"x1_loaded{n}") for n in range(NBX)]
            hi_done, lo_done = sem("hi_done"), sem("lo_done")
            iota_done, tok_done = sem("iota_done"), sem("tok_done")
            pick_done, pickT_ps, pickT_done = sem("pick_done"), sem("pickT_ps"), sem("pickT_done")
            ghi_ps, glo_ps, xehi_done, xelo_done = sem("ghi_ps"), sem("glo_ps"), sem("xehi_done"), sem("xelo_done")
            g_ps, u_ps, silu_done, hid_done = sem("g_ps"), sem("u_ps"), sem("silu_done"), sem("hid_done")
            down_ps, xe_done = sem("down_ps"), sem("xe_done")
            put_done, f_ps, est_done, eve_done, negm_done, ers_done = (
                sem(n) for n in ("put_done", "f_ps", "est_done", "eve_done", "negm_done", "ers_done"))
            emv_done, nmr_done, zn_done, res_done = (sem(n) for n in ("emv_done", "nmr_done", "zn_done", "res_done"))
            stored = [sem(f"stored{n}") for n in range(2)]

            def val(k, g, m):
                return add(k * g, m)

            def groups(eng, prologue, body):
                prologue()
                with eng.Fori(0, NG - 1) as g:
                    body(g, True)
                body(NG - 1, False)

            def rows_of(t, g, b):
                i = val(GB, g, b)
                v = t[i:i + 1] if isinstance(i, int) else t[bass.ds(i, 1)]
                return v.rearrange("b p t d -> (b p) t d")

            with nc.Block() as block:
                @block.sync
                def _(sp):
                    def load_xn(g, b):
                        if not isinstance(g, int) or g > 0 or b >= NBX:
                            sp.wait_ge(lo_done, val(GB, g, b - NBX + 1))
                            settled(sp)
                        sp.dma_start(xn_rows[:, b % NBX], rows_of(xn_dram, g, b)).then_inc(xn_loaded[b % NBX], 16)

                    def load_x1(g, b):
                        sp.wait_ge(res_done, val(GB, g, max(b - NBX + 1, 0) + 1))
                        settled(sp)
                        sp.dma_start(x1_rows[:, b % NBX], rows_of(x1_dram, g, b)).then_inc(x1_loaded[b % NBX], 16)

                    def prologue():
                        for n in range(2):
                            sp.sem_inc(stored[n], 1)
                        for b in range(GB):
                            load_xn(0, b)

                    def body(g, follows):
                        for b in range(NBX):
                            load_x1(g, b)
                        if follows:
                            for b in range(NBX + 1):
                                load_xn(g + 1, b)
                        for b in range(GB):
                            if follows and b + NBX + 1 < GB:
                                load_xn(g + 1, b + NBX + 1)
                            sp.wait_ge(res_done, val(GB, g, b + 2))
                            settled(sp)
                            i = val(GB, g, b)
                            dst = out[i:i + 1] if isinstance(i, int) else out[bass.ds(i, 1)]
                            sp.dma_start(dst.rearrange("b (t p) d -> (b p) t d", p=P), res[:, b % 2]).then_inc(stored[b % 2], 16)
                            if b + NBX < GB:
                                load_x1(g, b + NBX)

                    groups(sp, prologue, body)
                    for n in range(2):
                        sp.wait_ge(stored[n], 16 * (B // 2) + 1)

                @block.gpsimd
                def _(pool):
                    def split_lo(g, b):
                        pool.wait_ge(hi_done, val(GB, g, b + 1))
                        pool.tensor_tensor(out=xn_lo[:, b % 2], in0=xn_rows[:, b % NBX], in1=xn_hi[:, b % 2], op=ALU.subtract
                                           ).then_inc(lo_done, 1)

                    def rstd_of(g, b):
                        pool.wait_ge(nmr_done, val(GB, g, b + 1))
                        pool.wait_ge(emv_done, val(2 * GB, g, 2 * b + 3))
                        settled(pool)
                        pool.tensor_scalar(out=eve[:], in0=emv[:, b % 2, :, 1], scalar1=EPS, scalar2=None, op0=ALU.add).then_inc(eve_done, 1)
                        pool.tensor_scalar(out=negm[:], in0=emv[:, b % 2, :, 0], scalar1=-1.0, scalar2=None, op0=ALU.mult).then_inc(negm_done, 1)
                        pool.wait_ge(zn_done, val(2 * GB, g, 2 * max(b - 1, 0) + 1))
                        pool.wait_ge(eve_done, val(GB, g, b + 1))
                        pool.tensor_tensor(out=ers[:, b % 2], in0=eve[:], in1=neghalf[:], op=ALU.pow).then_inc(ers_done, 1)
                        pool.wait_ge(negm_done, val(GB, g, b + 1))
                        pool.wait_ge(ers_done, val(GB, g, b + 1))
                        pool.tensor_tensor(out=nmr[:, b % 2], in0=negm[:], in1=ers[:, b % 2], op=ALU.mult).then_inc(nmr_done, 1)

                    def residual(g, b):
                        pool.wait_ge(zn_done, val(2 * GB, g, 2 * b + 3))
                        pool.wait_ge(x1_loaded[b % NBX], val(16 * GB // NBX, g, 16 * (b // NBX) + 16))
                        pool.wait_ge(stored[b % 2], val(16 * GB // 2, g, 16 * (b // 2) + 1))
                        pool.tensor_tensor(out=res[:, b % 2], in0=zn[:, b % 2], in1=x1_rows[:, b % NBX], op=ALU.add).then_inc(res_done, 1)

                    def prologue():
                        pool.iota(iota[:], pattern=[[1, S]], base=0, channel_multiplier=0,
                                  allow_small_or_imprecise_dtypes=True).then_inc(iota_done, 1)
                        for one in (nmr_done, res_done):
                            pool.sem_inc(one, 1)
                        for b in range(GB):
                            split_lo(0, b)

                    def body(g, follows):
                        if follows:
                            for b in range(2):
                                split_lo(g + 1, b)
                        for b in range(GB):
                            if follows and b + 2 < GB:
                                split_lo(g + 1, b + 2)
                            rstd_of(g, b)
                            if b:
                                residual(g, b - 1)
                        residual(g, GB - 1)

                    groups(pool, prologue, body)

                @block.scalar
                def _(act):
                    def split_hi(g, b):
                        act.wait_ge(xn_loaded[b % NBX], val(16 * GB // NBX, g, 16 * (b // NBX) + 16))
                        if not isinstance(g, int) or g > 0 or b >= 2:
                            act.wait_ge(glo_ps, val(GB, g, b - 1))
                        nc.scalar.copy(xn_hi[:, b % 2], xn_rows[:, b % NBX]).then_inc(hi_done, 1)

                    def copy_pick(g, b):
                        act.wait_ge(pickT_ps, val(GB, g, b + 1))
                        if not isinstance(g, int) or g > 0 or b >= 2:
                            act.wait_ge(glo_ps, val(GB, g, b - 1))
                        nc.scalar.copy(pickT[:, b % 2], ps_pt[b % 2]).then_inc(pickT_done, 1)

                    def gathered_hi(g, b):
                        act.wait_ge(ghi_ps, val(GB, g, b + 1))
                        nc.scalar.copy(xeT_hi[:, :, b * CAP:(b + 1) * CAP], ps_g[b % 2][:].rearrange("p (e j) -> p e j", e=E)
                                       ).then_inc(xehi_done, 1)

                    def last_norm(g, b, follows):
                        act.wait_ge(nmr_done, val(GB, g, b + 2))
                        act.wait_ge(res_done, val(GB, g, max(b - 1, 0) + 1))
                        for t in range(ST):
                            nc.scalar.activation(zn[:, b % 2, t], sum_bank(b, follows)[:, t], ACT.Identity, bias=nmr[:, b % 2, t:t + 1],
                                                 scale=ers[:, b % 2, t:t + 1]).then_inc(zn_done, 1)

                    def gated(g, n):
                        act.wait_ge(g_ps, val(NU, g, n + 1))
                        if n >= 2 or not isinstance(g, int) or g > 0:
                            act.wait_ge(hid_done, val(NU, g, n - 1))
                        nc.scalar.activation(silu[:, n % 2], ps_g[n % 2][:], ACT.Silu).then_inc(silu_done, 1)

                    def prologue():
                        act.sem_inc(zn_done, 1)
                        for b in range(2):
                            split_hi(0, b)
                        copy_pick(0, 0)
                        for b in range(GB):
                            if b + 1 < GB:
                                copy_pick(0, b + 1)
                            gathered_hi(0, b)
                            if b + 2 < GB:
                                split_hi(0, b + 2)
                        for n in range(2):
                            gated(0, n)

                    def body(g, follows):
                        for n in range(2, NU):
                            gated(g, n)
                        if follows:
                            for b in range(2):
                                split_hi(g + 1, b)
                            copy_pick(g + 1, 0)
                        for b in range(GB):
                            if follows:
                                if b + 1 < GB:
                                    copy_pick(g + 1, b + 1)
                                gathered_hi(g + 1, b)
                                if b + 2 < GB:
                                    split_hi(g + 1, b + 2)
                            if b:
                                last_norm(g, b - 1, follows)
                        if follows:
                            for n in range(2):
                                gated(g + 1, n)
                        last_norm(g, GB - 1, follows)

                    groups(act, prologue, body)

                @block.vector
                def _(dve):
                    def copy_tokens(dst, src, g, n):
                        i = GB * g
                        v = src[:, i:i + GB] if isinstance(g, int) else src[:, bass.ds(i, GB)]
                        dve.tensor_copy(dst[:], v).then_inc(tok_done, 1)

                    def one_hot(dst, tok, b, done):
                        for m in range(M):
                            dve.tensor_scalar(out=dst[:, m], in0=iota[:], scalar1=tok[:, b, m:m + 1], scalar2=None,
                                              op0=ALU.is_equal).then_inc(done, 1)

                    def pick_rows(g, b):
                        if not isinstance(g, int) or g > 0 or b >= 2:
                            dve.wait_ge(pickT_ps, val(GB, g, b - 1))
                        one_hot(pick[:, b % 2], tok_pick, b, pick_done)

                    def put_rows(g, b):
                        if b >= NBX:
                            dve.wait_ge(f_ps, val(GB, g, b - NBX + 1))
                        one_hot(put[:, b % NBX], tok_put, b, put_done)

                    def gathered_lo(g, b):
                        dve.wait_ge(glo_ps, val(GB, g, b + 1))
                        dve.tensor_copy(xeT_lo[:, :, b * CAP:(b + 1) * CAP], ps_u[b % 2][:].rearrange("p (e j) -> p e j", e=E)
                                        ).then_inc(xelo_done, 1)

                    def last_stats(g, b, follows):
                        dve.wait_ge(emv_done, val(2 * GB, g, 2 * max(b - 1, 0) + 1))
                        dve.wait_ge(f_ps, val(GB, g, b + 1))
                        for t in range(ST):
                            dve.bn_stats(out=est[:, b % 2, t], in_=sum_bank(b, follows)[:, t]).then_inc(est_done, 1)

                    def last_aggr(g, b):
                        dve.wait_ge(est_done, val(2 * GB, g, 2 * b + 2))
                        dve.wait_ge(nmr_done, val(GB, g, max(b - 1, 0) + 1))
                        settled(dve)
                        for t in range(ST):
                            dve.bn_aggr(out=emv[:, b % 2, t], in_=est[:, b % 2, t]).then_inc(emv_done, 1)

                    def weighted(g, m):
                        for n in range(2):
                            bs = slice(n * GB // 2, (n + 1) * GB // 2)
                            dve.wait_ge(down_ps, val(2 * M, g, 2 * m + n + 1))
                            dve.tensor_tensor(out=xe[:, m, bs], in0=ps_d[:, bs], in1=gat[:, bs, m:m + 1].broadcast_to([P, GB // 2, D]),
                                              op=ALU.mult).then_inc(xe_done, 1)

                    def prologue():
                        dve.sem_inc(emv_done, 1)
                        dve.wait_ge(iota_done, 1)
                        copy_tokens(tok_pick, slot_token, 0, 1)
                        dve.wait_ge(tok_done, 1)
                        for b in range(2):
                            pick_rows(0, b)
                        for b in range(GB):
                            if b + 2 < GB:
                                pick_rows(0, b + 2)
                            gathered_lo(0, b)

                    def body(g, follows):
                        copy_tokens(tok_put, slot_token, g, 2)
                        copy_tokens(gat, slot_gate, g, 3)
                        dve.wait_ge(tok_done, val(3, g, 3))
                        for n in range(NU):
                            e, it = n // IT, n % IT
                            dve.wait_ge(silu_done, val(NU, g, n + 1))
                            dve.wait_ge(u_ps, val(NU, g, n + 1))
                            if e >= NBH and it == 0:
                                dve.wait_ge(down_ps, val(2 * M, g, (e - NBH) // 2 * 2 + 2))
                            dve.tensor_tensor(out=hid[:, e % NBH, it], in0=silu[:, n % 2], in1=ps_u[n % 2][:], op=ALU.mult
                                              ).then_inc(hid_done, 1)
                            if n % (2 * IT) == 3 and n > IT:
                                weighted(g, n // (2 * IT) - 1)
                            if n % (2 * IT) == 5:
                                put_rows(g, n // (2 * IT))
                            if n == NU - 8 and follows:
                                copy_tokens(tok_pick, slot_token, g + 1, 1)
                            if n == NU - 6 and follows:
                                dve.wait_ge(tok_done, val(3, g, 4))
                                pick_rows(g + 1, 0)
                            if n == NU - 4 and follows:
                                pick_rows(g + 1, 1)
                        weighted(g, M - 1)
                        for b in range(GB):
                            if follows:
                                if b + 2 < GB:
                                    pick_rows(g + 1, b + 2)
                                gathered_lo(g + 1, b)
                            last_stats(g, b, follows)
                            if b + NBX < GB:
                                put_rows(g, b + NBX)
                            last_aggr(g, b)

                    groups(dve, prologue, body)

                @block.tensor
                def _(pe):
                    def transpose_pick(g, b):
                        pe.wait_ge(pick_done, val(GB * M, g, M * (b + 1)))
                        if not isinstance(g, int) or g > 0 or b >= 2:
                            pe.wait_ge(pickT_done, val(GB, g, b - 1))
                        for t in range(ST):
                            for m in range(M):
                                last = nc.tensor.transpose(ps_pt[b % 2][:, t, m * P:(m + 1) * P],
                                                           pick[:, b % 2, m, t * P:(t + 1) * P], identb[:])
                        last.then_inc(pickT_ps, 1)

                    def gather(g, b):
                        pe.wait_ge(pickT_done, val(GB, g, b + 1))
                        pe.wait_ge(lo_done, val(GB, g, b + 1))
                        if not isinstance(g, int) or g > 0 or b >= 2:
                            pe.wait_ge(xehi_done, val(GB, g, b - 1))
                            pe.wait_ge(xelo_done, val(GB, g, b - 1))
                        for bank, part, done in ((ps_g, xn_hi, ghi_ps), (ps_u, xn_lo, glo_ps)):
                            for t in range(ST):
                                last = nc.tensor.matmul(bank[b % 2][:], part[:, b % 2, t], pickT[:, b % 2, t],
                                                        start=t == 0, stop=t == ST - 1)
                            last.then_inc(done, 1)

                    def gate_up(g, n):
                        e, it = n // IT, n % IT
                        if n >= 2:
                            pe.wait_ge(hid_done, val(NU, g, n - 1))
                        for k, (bank, done) in enumerate(((ps_g, g_ps), (ps_u, u_ps))):
                            hi, lo = (w[k][:, e, it * P:(it + 1) * P] for w in (w_hi, w_lo))
                            nc.tensor.matmul(bank[n % 2][:], hi, xeT_hi[:, e], start=True, stop=False)
                            nc.tensor.matmul(bank[n % 2][:], hi, xeT_lo[:, e], start=False, stop=False)
                            nc.tensor.matmul(bank[n % 2][:], lo, xeT_hi[:, e], start=False, stop=True).then_inc(done, 1)

                    def down(g, m):
                        pe.wait_ge(hid_done, val(NU, g, 2 * IT * (m + 1)))
                        if not m:
                            pe.wait_ge(zn_done, val(2 * GB, g, 1))
                        for b in range(GB):
                            if m and b % (GB // 2) == 0:
                                pe.wait_ge(xe_done, val(2 * M, g, 2 * m - 1 + b // (GB // 2)))
                            for it in range(IT):
                                for half in range(2):
                                    last = nc.tensor.matmul(ps_d[half * CAP:(half + 1) * CAP, b],
                                                            hid[:, (2 * m + half) % NBH, it, b * CAP:(b + 1) * CAP],
                                                            wd_sb[:, 2 * m + half, it],
                                                            start=it == 0, stop=it == IT - 1)
                            if b % (GB // 2) == GB // 2 - 1:
                                last.then_inc(down_ps, 1)

                    def scatter(g, b, follows):
                        pe.wait_ge(put_done, val(GB * M, g, M * (b + 1)))
                        n = 2 if follows else 4
                        if b >= n:
                            pe.wait_ge(zn_done, val(2 * GB, g, 2 * (b - n) + 3))
                        for t in range(ST):
                            for m in range(M):
                                last = nc.tensor.matmul(sum_bank(b, follows)[:, t], put[:, b % NBX, m, t * P:(t + 1) * P],
                                                        xe[:, m, b], start=m == 0, stop=m == M - 1)
                        last.then_inc(f_ps, 1)

                    def prologue():
                        transpose_pick(0, 0)
                        for b in range(GB):
                            if b + 1 < GB:
                                transpose_pick(0, b + 1)
                            gather(0, b)

                    def body(g, follows):
                        pe.wait_ge(xehi_done, val(GB, g, GB))
                        pe.wait_ge(xelo_done, val(GB, g, GB))
                        for n in range(NU):
                            gate_up(g, n)
                            if n % (2 * IT) == 1 and n > IT:
                                down(g, n // (2 * IT) - 1)
                        if follows:
                            transpose_pick(g + 1, 0)
                        down(g, M - 1)
                        if follows:
                            gather(g + 1, 0)
                        pe.wait_ge(xe_done, val(2 * M, g, 2 * M))
                        for b in range(GB):
                            if follows and b:
                                gather(g + 1, b)
                            if follows and b + 1 < GB:
                                transpose_pick(g + 1, b + 1)
                            scatter(g, b, follows)

                    groups(pe, prologue, body)


def kernel(**inputs):
    import numpy as np
    import concourse.bacc as bacc
    from concourse import mybir as mb
    from concourse.bass_utils import run_bass_kernel_spmd

    a = {n.split("_", 1)[1]: np.asarray(v) for n, v in inputs.items()}

    def by_lane(w):
        return w.reshape(*w.shape[:-1], H, DH).swapaxes(-1, -2).reshape(w.shape)

    pos = np.arange(S, dtype=np.float32)[:, None]
    div = np.exp(np.arange(0, D, 2, dtype=np.float32) * np.float32(-np.log(10000.0) / D))
    pe_tab = np.zeros((S, D), np.float32)
    pe_tab[:, 0::2] = np.sin(pos * div)
    pe_tab[:, 1::2] = np.cos(pos * div)
    arrays = {
        "x": a["attn_x"], "Wq": by_lane(a["attn_Wq"]), "bq": by_lane(a["attn_bq"]), "Wk": by_lane(a["attn_Wk"]),
        "bk": by_lane(a["attn_bk"]), "Wv": a["attn_Wv"], "bv": a["attn_bv"], "Wo": a["attn_Wo"], "bo": a["attn_bo"],
        "gamma": a["attn_gamma"], "beta": a["attn_beta"], "gate": a["ffn_gate_w"].T,
        "wg": a["ffn_w_gate"].transpose(0, 2, 1), "wu": a["ffn_w_up"].transpose(0, 2, 1),
        "wd": a["ffn_w_down"].transpose(0, 2, 1), "pe_tab": pe_tab,
    }
    arrays = {n: np.ascontiguousarray(v) for n, v in arrays.items()}
    nc = bacc.Bacc("TRN2", target_bir_lowering=False, num_devices=1)
    args = [nc.dram_tensor(n, v.shape, mb.dt.from_np(v.dtype), kind="ExternalInput").ap() for n, v in arrays.items()]
    out = nc.dram_tensor("out", (B, S, D), mb.dt.float32, kind="ExternalOutput").ap()
    build(nc, *args, out)
    r = run_bass_kernel_spmd(nc, [arrays], core_ids=[0])
    return r.results[0]["out"]
```

```python
import concourse.bass as bass
from concourse import mybir
from contextlib import ExitStack

B, S, D, H, E, I = 32, 256, 128, 16, 8, 512
DH = D // H
CAP = S // E * 2
P = 128
ST = S // P
IT = I // P
EPS = 1e-5
SCALE = float(DH) ** -0.5

QPART = (0, 0, 1, 1, 0, 2)
KPART = (0, 1, 0, 1, 2, 0)
NPROD = len(QPART)
MROW = NPROD * DH
KROWS = MROW + 3
ONES = 32
PAIR = 1 + 0x3F80 / 2 ** 23

NB4 = 4
LOOP0, NLOOP = 4, 6
FIRST, LAST = -4, B + 2
WARM_STEP, WARM = 0, 10
GB = 8
NG = B // GB
M = E // 2


def add(q, k):
    return q + k if k else q


def live(q, c):
    return not isinstance(q, int) or 0 <= 4 * q + c < B


def has_prior(q, c, n):
    return not isinstance(q, int) or 4 * q + c >= n


def batch(q, c, d):
    return add(q, (c + d) // 4), (c + d) % 4


def nth(q, c, k, m):
    return add(4 * k * q, k * c + m)


MISC = (("xnT", -3), ("logit", -3), ("OT", -1), ("onT", -1), ("Wo", -1), ("hT", 3), ("QK", 3), ("nmT", 1), ("V", 3))


def misc_use(q, c, name):
    if not isinstance(q, int):
        return add(4 * len(MISC) * q, len(MISC) * (c - LOOP0) + misc_use(0, LOOP0, name))
    s, n = 4 * q + c, 0
    for t in range(FIRST, s + 1):
        for use, d in MISC:
            if t == s and use == name:
                return n
            n += 0 <= t + d < B
    raise ValueError(name)


def build(nc, x, Wq, bq, Wk, bk, Wv, bv, Wo, bo, gamma, beta, gate, wg, wu, wd, pe_tab, out):
    F32, F32R, BF16, U32 = mybir.dt.float32, mybir.dt.float32r, mybir.dt.bfloat16, mybir.dt.uint32
    ALU, ACT, AX = mybir.AluOpType, mybir.ActivationFunctionType, mybir.AxisListType
    top = ExitStack()
    names = [0]

    def sem(name):
        return top.enter_context(nc.semaphore(name))

    def steps(eng, run):
        for s in range(FIRST, LOOP0):
            run(s // 4, s % 4)
        with eng.Fori(0, NLOOP) as g:
            for j in range(4):
                run(add(g, (LOOP0 + j) // 4), (LOOP0 + j) % 4)
        for s in range(LOOP0 + 4 * NLOOP, LAST + 1):
            run(s // 4, s % 4)

    with top:
        def sb(name, shape, dt=F32, ctx=top):
            return ctx.enter_context(nc.sbuf_tensor(name, shape, dt))

        def ps(name, shape, dt=F32, ctx=top):
            return ctx.enter_context(nc.psum_tensor(name, shape, dt))

        x1_dram = nc.dram_tensor("x1_scratch", (B, P, ST, D), F32, kind="Internal").ap()
        xn_dram = nc.dram_tensor("xn_scratch", (B, P, ST, D), F32, kind="Internal").ap()

        wg_sb = sb("wg_sb", [P, E, I])
        wu_sb = sb("wu_sb", [P, E, I])
        wd_sb = sb("wd_sb", [P, E, IT, D])
        ident = sb("ident", [P, P])
        identb = sb("identb", [P, P], BF16)
        logits = sb("logits", [P, ST, B, E])
        slot_token = sb("slot_token", [P, B, M])
        slot_gate = sb("slot_gate", [P, B, M])
        neghalf = sb("neghalf", [P, ST])
        iota = sb("iota", [P, S])
        w_loaded = sem("w_loaded")
        consts = sem("consts")
        ones_done = sem("ones_done")
        carried = sem("carried")

        def settled(eng):
            eng.sem_inc(carried, 1)

        R = B * E // P
        RB = B // R
        scan_late = logits[:].rearrange("p t b e -> p (t b e)")[:, 0:S]
        top_gate_late = sb("top_gate_late", [P, 2, CAP])
        top_idx_late = sb("top_idx_late", [P, CAP], U32)
        top_token_late = sb("top_token_late", [P, 2, CAP])
        ROUNDS = CAP // 8

        class Half:
            def __init__(self, r, mem):
                self.rows = slice(r * RB, (r + 1) * RB)
                self.ex = mem(f"ex{r}", [P, ST, RB, E])
                self.aff = mem(f"aff{r}", [P, ST, RB, E])
                self.row = mem(f"row{r}", [P, ST, RB])
                self.rowr = mem(f"rowr{r}", [P, ST, RB])
                self.soft, self.exp_done = sem(f"soft{r}"), sem(f"exp{r}_done")

            def wide(self, v):
                return v[:].rearrange("p t (b a) -> p t b a", a=1).broadcast_to([P, ST, RB, E])

            def less_max(self, dve):
                lv = logits[:, :, self.rows, :]
                dve.tensor_reduce(out=self.row[:], in_=lv, axis=AX.X, op=ALU.max).then_inc(self.soft, 1)
                dve.wait_ge(self.soft, 1)
                dve.tensor_tensor(out=lv, in0=lv, in1=self.wide(self.row), op=ALU.subtract).then_inc(self.soft, 1)

            def exponentials(self, act):
                act.wait_ge(self.soft, 2)
                nc.scalar.activation(self.ex[:], logits[:, :, self.rows, :], ACT.Exp).then_inc(self.exp_done, 1)

            def over_sum(self, dve):
                dve.wait_ge(self.exp_done, 1)
                dve.tensor_reduce(out=self.row[:], in_=self.ex[:], axis=AX.X, op=ALU.add).then_inc(self.soft, 1)
                dve.wait_ge(self.soft, 3)
                dve.reciprocal(self.rowr[:], self.row[:]).then_inc(self.soft, 1)
                dve.wait_ge(self.soft, 4)
                dve.tensor_tensor(out=self.aff[:], in0=self.ex[:], in1=self.wide(self.rowr), op=ALU.mult).then_inc(self.soft, 1)

            def transposed(self, pe, dst, done):
                pe.wait_ge(self.soft, 5)
                for t in range(ST):
                    last = nc.tensor.transpose(dst[:, t * P:(t + 1) * P], self.aff[:, t].rearrange("p b e -> p (b e)"), ident[:])
                last.then_inc(done, 1)

        def top_round(dve, done, before, n, scan, gates, idx):
            eight = slice(8 * n, 8 * n + 8)
            if before:
                dve.wait_ge(done, before)
            dve.max(out=gates[:, 0, eight], in_=scan).then_inc(done, 1)
            dve.wait_ge(done, before + 1)
            dve.max_index(out=idx[:, eight], in_max=gates[:, 0, eight], in_values=scan).then_inc(done, 1)
            dve.wait_ge(done, before + 2)
            dve.match_replace(out=scan, in_to_replace=gates[:, 0, eight], in_values=scan, imm_value=-1.0).then_inc(done, 1)

        def top_copies(dve, done, before, gates, idx, token):
            dve.wait_ge(done, before)
            dve.tensor_copy(gates[:, 1], gates[:, 0]).then_inc(done, 1)
            for n in range(2):
                dve.tensor_copy(token[:, n], idx[:]).then_inc(done, 1)

        def slot_copies(dve, done, r, src):
            for n, dst in enumerate((slot_token, slot_gate)):
                for half in range(2):
                    rows = slice(half * CAP, (half + 1) * CAP)
                    v = src[rows, n].rearrange("p (b m two) -> p b m two", m=M, two=2)
                    dve.tensor_copy(dst[rows, r * RB:(r + 1) * RB], v[:, :, :, half]).then_inc(done, 1)

        with ExitStack() as actx:
            def sa(name, shape, dt=F32):
                return sb(name, shape, dt, actx)

            qks = sa("qks", [P, NB4, H, 2, S], BF16)
            qs, ks = qks[:, :, :, 0], qks[:, :, :, 1]
            vst = sa("vst", [P, NB4, ST, H, 32])
            probs = sa("probs", [P, 4, 4, S])
            h_bo = sa("h_bo", [P, NB4, ST, D])
            x_in = sa("x_in", [P, 2, ST, D])
            x_res = sa("x_res", [P, 2, ST, D])
            xn1 = sa("xn1", [P, ST, D])
            h = sa("h", [P, 2, ST, D])
            hT = sa("hT", [P, S])
            qk = sa("qk", [P, 2, S])
            qk_part = sa("qk_part", [P, 6, S], BF16)
            qk_rest = sa("qk_rest", [P, 2, S])
            nm = sa("nm", [P, 2, ST, H])
            nm_part = sa("nm_part", [P, ST, 3, H], BF16)
            nm_rest = sa("nm_rest", [P, ST, H])
            nmT = sa("nmT", [3 * H, S], BF16)
            o_aug = sa("o_aug", [P, 2, S])
            o_rec = sa("o_rec", [P, ST * H])
            o_norm = sa("o_norm", [P, ST, D])
            onT = sa("onT", [P, S])
            y = sa("y", [P, ST, D])
            z2 = sa("z2", [P, ST, D])
            z2g = sa("z2g", [P, ST, D])
            z2b = sa("z2b", [P, ST, D])
            z3 = sa("z3", [P, ST, D])
            x1 = sa("x1", [P, 2, ST, D])
            xn2 = sa("xn2", [P, 2, ST, D])
            xnT = sa("xnT", [P, S])
            stats = [sa(f"stats{n}", [P, ST, 6]) for n in range(4)]
            ks_f32 = ks.bitcast(F32)
            mv = [sa(f"mv{n}", [P, ST, 2]) for n in range(4)]
            veps = [sa(f"veps{n}", [P, ST]) for n in range(4)]
            rstd = [sa(f"rstd{n}", [P, ST]) for n in range(4)]
            negmean = {n: sa(f"negmean{n}", [P, ST]) for n in (0, 3)}
            nmrstd = {n: sa(f"nmrstd{n}", [P, ST]) for n in (0, 3)}
            wq_sb, wk_sb, wv_sb, wo_sb = (sa(n, [P, D]) for n in ("wq_sb", "wk_sb", "wv_sb", "wo_sb"))
            gate_sb = sa("gate_sb", [P, E])
            bq_sb, bk_sb = sa("bq_sb", [P, 1]), sa("bk_sb", [P, 1])
            bo_sb, gam_sb, bet_sb = (sa(n, [P, D]) for n in ("bo_sb", "gam_sb", "bet_sb"))
            pe_sb = sa("pe_sb", [P, ST, D])
            pebo = sa("pebo", [P, ST, D])
            bv_col, bv_wide, bvo = sa("bv_col", [P, 1]), sa("bv_wide", [P, D]), sa("bvo", [P, D])

            half0 = Half(0, sa)
            scan = sa("scan", [P, S])
            top_gate = sa("top_gate", [P, 2, CAP])
            top_idx = sa("top_idx", [P, CAP], U32)
            top_token = sa("top_token", [P, 2, CAP])
            aff_ps, top_done, top_ps, slots_done = sem("aff_ps"), sem("top_done"), sem("top_ps"), sem("slots_done")

            def on(q, c, step):
                return isinstance(q, int) and 4 * q + c == step

            ps_s = [ps(f"ps_s{n}", [P, 2, S], F32, actx) for n in range(2)]
            ps_st = [ps(f"ps_st{n}", [P, 4, S], F32, actx) for n in range(2)]
            ps_av = ps("ps_av", [P, 2, S], F32, actx)
            misc = ps("misc", [P, 512], F32, actx)

            small_loaded = sem("small_loaded")
            x_loaded = [sem(f"x_loaded{n}") for n in range(2)]
            res_loaded = [sem(f"res_loaded{n}") for n in range(2)]
            spread = [sem(f"spread{n}") for n in range(NB4)]
            nm_spread = [sem(f"nm_spread{n}") for n in range(NB4)]
            x1_stored = [sem(f"x1_stored{n}") for n in range(2)]
            xn_stored = [sem(f"xn_stored{n}") for n in range(2)]
            misc_full, misc_free = sem("misc_full"), sem("misc_free")
            s_done, max_done = sem("s_done"), sem("max_done")
            st_done, exp_done, av_done = sem("st_done"), sem("exp_done"), sem("av_done")
            oaug_done, orec_done = sem("oaug_done"), sem("orec_done")
            stats_done = [sem(f"stats_done{n}") for n in range(4)]
            mv_done = [sem(f"mv_done{n}") for n in range(4)]
            veps_done = [sem(f"veps_done{n}") for n in range(4)]
            rstd_done = [sem(f"rstd_done{n}") for n in range(4)]
            negmean_done = {n: sem(f"negmean_done{n}") for n in (0, 3)}
            nmrstd_done = {n: sem(f"nmrstd_done{n}") for n in (0, 3)}
            norm_done = [sem(f"norm_done{n}") for n in range(4)]
            h_done, hbo_done = sem("h_done"), sem("hbo_done")
            qk_done, part0_done, rest_done, part1_done, part2_done = (sem(f"qk{n}_done") for n in range(5))
            bvo_done, bvo_ps = sem("bvo_done"), sem("bvo_ps")
            v_done = sem("v_done")
            nm0_done, nmr_done, nm1_done, nm2_done = (sem(f"nm{n}_done") for n in range(4))
            gam_done, bet_done, x1_done = sem("gam_done"), sem("bet_done"), sem("x1_done")
            pebo_done = sem("pebo_done")
            NSMALL = 12

            def x_rows(src, q, c):
                if isinstance(q, int):
                    v = src[4 * q + c:4 * q + c + 1]
                else:
                    v = src[bass.ds(add(4 * q, c), 1)]
                return v.rearrange("b (t p) d -> (b p) t d", p=P)

            def scratch(dst, q, c):
                if isinstance(q, int):
                    v = dst[4 * q + c:4 * q + c + 1]
                else:
                    v = dst[bass.ds(add(4 * q, c), 1)]
                return v.rearrange("b p t d -> (b p) t d")

            with nc.Block() as block:
                @block.sync
                def _(sp):
                    sp.dma_start(x_in[:, 0], x_rows(x, 0, 0)).then_inc(x_loaded[0], 16)
                    for dst, src in ((wq_sb, Wq), (wk_sb, Wk), (wv_sb, Wv), (wo_sb, Wo), (gate_sb, gate)):
                        sp.dma_start(dst[:], src).then_inc(small_loaded, 16)
                    for dst, src in ((bq_sb, bq), (bk_sb, bk), (bv_col, bv)):
                        sp.dma_start(dst[:], src.rearrange("(d a) -> d a", a=1)).then_inc(small_loaded, 16)
                    for dst, src in ((bo_sb, bo), (gam_sb, gamma), (bet_sb, beta)):
                        sp.dma_start(dst[:], src.rearrange("(a d) -> a d", a=1).broadcast_to([P, D])).then_inc(small_loaded, 16)
                    sp.dma_start(pe_sb[:], pe_tab.rearrange("(t p) d -> p t d", p=P)).then_inc(small_loaded, 16)

                    def run(q, c):
                        b4, c4 = batch(q, c, 4)
                        if live(b4, c4) and has_prior(b4, c4, 1):
                            if has_prior(b4, c4, 2):
                                sp.wait_ge(norm_done[0], nth(b4, c4, 2, -2))
                            settled(sp)
                            sp.dma_start(x_in[:, c4 % 2], x_rows(x, b4, c4)).then_inc(x_loaded[c4 % 2], 16)
                        b, cc = batch(q, c, -1)
                        if live(b, cc):
                            if has_prior(b, cc, 2):
                                sp.wait_ge(x1_done, nth(b, cc, 1, -1))
                            settled(sp)
                            sp.dma_start(x_res[:, cc % 2], x_rows(x, b, cc)).then_inc(res_loaded[cc % 2], 16)
                        b, cc = batch(q, c, -2)
                        if live(b, cc):
                            sp.wait_ge(x1_done, nth(b, cc, 1, 1))
                            settled(sp)
                            sp.dma_start(scratch(x1_dram, b, cc), x1[:, cc % 2]).then_inc(x1_stored[cc % 2], 16)
                        b, cc = batch(q, c, 1)
                        if live(b, cc):
                            sp.wait_ge(misc_free, add(misc_use(q, c, "nmT"), 1))
                            sp.dma_start(qs[MROW:MROW + 3, cc], nmT[:]).then_inc(nm_spread[cc], 16)
                        b, cc = batch(q, c, 3)
                        if live(b, cc):
                            if has_prior(b, cc, 4):
                                sp.wait_ge(st_done, nth(b, cc, 8, -24))
                                settled(sp)
                            else:
                                sp.wait_ge(ones_done, NB4)
                            newest = -1
                            for n, (qpart, kpart) in enumerate(zip(QPART, KPART)):
                                if max(qpart, kpart) > newest:
                                    newest = max(qpart, kpart)
                                    sp.wait_ge((part0_done, part1_done, part2_done)[newest], nth(b, cc, 1, 1))
                                    settled(sp)
                                sp.dma_start(qks[n * DH:(n + 1) * DH, cc],
                                             qk_part[:, qpart:4 + kpart:3 + kpart - qpart]).then_inc(spread[cc], 16)
                        b, cc = batch(q, c, -2)
                        if live(b, cc):
                            sp.wait_ge(norm_done[3], nth(b, cc, 2, 2))
                            settled(sp)
                            sp.dma_start(scratch(xn_dram, b, cc), xn2[:, cc % 2]).then_inc(xn_stored[cc % 2], 16)

                    steps(sp, run)
                    for n in range(2):
                        sp.wait_ge(x1_stored[n], 16 * (B // 2))
                        sp.wait_ge(xn_stored[n], 16 * (B // 2))

                @block.gpsimd
                def _(pool):
                    pool.memset(ident[:], 0.0).then_inc(consts, 1)
                    pool.memset(identb[:], 0.0).then_inc(consts, 1)
                    pool.memset(neghalf[:], -0.5).then_inc(consts, 1)
                    pool.wait_ge(consts, 2)
                    for m in (ident, identb):
                        pool.affine_select(out=m[:], in_=m[:], compare_op=ALU.not_equal, fill=1.0, base=0,
                                           pattern=[[-1, P]], channel_multiplier=1).then_inc(consts, 1)
                    pool.memset(vst[:], 0.0).then_inc(v_done, 1)
                    pool.iota(iota[:], pattern=[[1, S]], base=0, channel_multiplier=0,
                              allow_small_or_imprecise_dtypes=True).then_inc(consts, 1)
                    pool.wait_ge(small_loaded, 16 * NSMALL)
                    pool.wait_ge(bvo_done, 2)
                    for t in range(ST):
                        pool.tensor_tensor(out=pebo[:, t], in0=pe_sb[:, t], in1=bvo[:], op=ALU.add).then_inc(pebo_done, 1)
                    pool.wait_ge(pebo_done, ST)

                    def rsqrt(n, b, c):
                        if has_prior(b, c, 1):
                            pool.wait_ge(norm_done[n], nth(b, c, 2, 0))
                        pool.wait_ge(mv_done[n], nth(b, c, 2, 2))
                        settled(pool)
                        pool.tensor_scalar(out=veps[n][:], in0=mv[n][:, :, 1], scalar1=EPS, scalar2=None, op0=ALU.add
                                           ).then_inc(veps_done[n], 1)
                        if n in nmrstd:
                            pool.tensor_scalar(out=negmean[n][:], in0=mv[n][:, :, 0], scalar1=-1.0, scalar2=None, op0=ALU.mult
                                               ).then_inc(negmean_done[n], 1)
                        pool.wait_ge(veps_done[n], nth(b, c, 1, 1))
                        pool.tensor_tensor(out=rstd[n][:], in0=veps[n][:], in1=neghalf[:], op=ALU.pow
                                           ).then_inc(rstd_done[n], 1)
                        if n in nmrstd:
                            pool.wait_ge(negmean_done[n], nth(b, c, 1, 1))
                            pool.wait_ge(rstd_done[n], nth(b, c, 1, 1))
                            pool.tensor_tensor(out=nmrstd[n][:], in0=negmean[n][:], in1=rstd[n][:], op=ALU.mult
                                               ).then_inc(nmrstd_done[n], 1)

                    def run(q, c):
                        b2, c2 = batch(q, c, -2)
                        b3, c3 = batch(q, c, 3)
                        b1, c1 = batch(q, c, -1)
                        bm, cm = batch(q, c, 1)
                        if live(b3, c3):
                            rsqrt(0, b3, c3)
                        if live(b2, c2):
                            rsqrt(2, b2, c2)
                        if live(b3, c3):
                            pool.wait_ge(norm_done[0], nth(b3, c3, 2, 2))
                            if has_prior(b3, c3, 2):
                                pool.wait_ge(qk_done, nth(b3, c3, 1, -1))
                            pool.tensor_tensor(out=h[:, c3 % 2], in0=xn1[:], in1=pe_sb[:], op=ALU.add
                                               ).then_inc(h_done, 1)
                        if live(b2, c2):
                            pool.wait_ge(norm_done[2], nth(b2, c2, 2, 2))
                            pool.wait_ge(res_loaded[c2 % 2], add(32 * b2, 16 * (c2 // 2) + 16))
                            if has_prior(b2, c2, 2):
                                pool.wait_ge(x1_stored[c2 % 2], add(32 * b2, 16 * (c2 // 2)))
                                pool.wait_ge(norm_done[3], nth(b2, c2, 2, -2))
                            pool.tensor_tensor(out=x1[:, c2 % 2], in0=z3[:], in1=x_res[:, c2 % 2], op=ALU.add
                                               ).then_inc(x1_done, 1)
                        if live(b2, c2):
                            rsqrt(3, b2, c2)
                        if live(bm, cm):
                            v = nm[:, cm % 2]
                            pool.wait_ge(max_done, nth(bm, cm, 16, 16))
                            if has_prior(bm, cm, 1):
                                pbm, pcm = batch(bm, cm, -1)
                                pool.wait_ge(nm_spread[pcm], add(16 * pbm, 16))
                            settled(pool)
                            pool.tensor_copy(nm_part[:, :, 0], v).then_inc(nm0_done, 1)
                            pool.wait_ge(nm0_done, nth(bm, cm, 1, 1))
                            pool.tensor_tensor(out=nm_rest[:], in0=v, in1=nm_part[:, :, 0], op=ALU.subtract).then_inc(nmr_done, 1)
                            pool.wait_ge(nmr_done, nth(bm, cm, 1, 1))
                            settled(pool)
                            pool.tensor_copy(nm_part[:, :, 1], nm_rest[:]).then_inc(nm1_done, 1)
                            pool.wait_ge(nm1_done, nth(bm, cm, 1, 1))
                            pool.tensor_tensor(out=nm_part[:, :, 2], in0=nm_rest[:], in1=nm_part[:, :, 1],
                                               op=ALU.subtract).then_inc(nm2_done, 1)
                        if live(b3, c3):
                            if has_prior(b3, c3, 4):
                                pool.wait_ge(misc_free, add(misc_use(q, c, "Wo"), 1))
                            pool.tensor_tensor(out=h_bo[:, c3], in0=xn1[:], in1=pebo[:], op=ALU.add
                                               ).then_inc(hbo_done, 1)
                        if live(b1, c1):
                            rsqrt(1, b1, c1)
                        if live(b3, c3):
                            pool.wait_ge(part0_done, nth(b3, c3, 1, 1))
                            pool.tensor_tensor(out=qk_rest[:], in0=qk[:], in1=qk_part[:, 0::3], op=ALU.subtract
                                               ).then_inc(rest_done, 1)
                        if live(b1, c1):
                            pool.wait_ge(norm_done[1], nth(b1, c1, 2, 2))
                            for t in range(ST):
                                pool.tensor_tensor(out=z2g[:, t], in0=z2[:, t], in1=gam_sb[:], op=ALU.mult).then_inc(gam_done, 1)
                            pool.wait_ge(gam_done, nth(b1, c1, 2, 2))
                            if has_prior(b1, c1, 1):
                                pool.wait_ge(norm_done[2], nth(b1, c1, 2, 0))
                            for t in range(ST):
                                pool.tensor_tensor(out=z2b[:, t], in0=z2g[:, t], in1=bet_sb[:], op=ALU.add).then_inc(bet_done, 1)
                        if live(b3, c3):
                            pool.wait_ge(part1_done, nth(b3, c3, 1, 1))
                            pool.tensor_tensor(out=qk_part[:, 2::3], in0=qk_rest[:], in1=qk_part[:, 1::3], op=ALU.subtract
                                               ).then_inc(part2_done, 1)

                    steps(pool, run)

                @block.scalar
                def _(act):
                    def load_expert(e):
                        act.dma_start(wg_sb[:, e], wg[e]).then_inc(w_loaded, 16)
                        act.dma_start(wu_sb[:, e], wu[e]).then_inc(w_loaded, 16)
                        act.dma_start(wd_sb[:, e], wd[e].rearrange("(t p) d -> p t d", p=P)).then_inc(w_loaded, 16)

                    def slot(q, c, u):
                        if live(q, c):
                            n = nth(q, c, 8, u)
                            act.wait_ge(st_done, add(n, 1))
                            if u >= 4 or has_prior(q, c, 1):
                                act.wait_ge(av_done, nth(q, c, 8, u - 3))
                            nc.scalar.activation(probs[:, u % 4], ps_st[u % 2][:], ACT.Exp, scale=SCALE).then_inc(exp_done, 1)

                    def norm_apply(n, b, c, dst, src):
                        act.wait_ge(nmrstd_done[n], nth(b, c, 1, 1))
                        for t in range(ST):
                            nc.scalar.activation(dst[:, t], src[:, t], ACT.Identity, bias=nmrstd[n][:, t:t + 1],
                                                 scale=rstd[n][:, t:t + 1]).then_inc(norm_done[n], 1)

                    def run(q, c):
                        b1, c1 = batch(q, c, -1)
                        b2, c2 = batch(q, c, -2)
                        b3, c3 = batch(q, c, 3)
                        br, cr = batch(q, c, -3)
                        if isinstance(q, int) and 0 <= 4 * q + c - FIRST < E:
                            act.wait_ge(small_loaded, 16 * NSMALL)
                            load_expert(4 * q + c - FIRST)
                        if live(br, cr):
                            act.wait_ge(misc_full, add(misc_use(q, c, "xnT"), 1))
                            nc.scalar.copy(xnT[:], misc[:, 0:S]).then_inc(misc_free, 1)
                        slot(q, c, 0)
                        if live(b1, c1):
                            act.wait_ge(av_done, nth(b1, c1, 8, 8))
                            nc.scalar.copy(o_aug[:], ps_av[:]).then_inc(oaug_done, 1)
                        if live(br, cr):
                            act.wait_ge(misc_full, add(misc_use(q, c, "logit"), 1))
                            if isinstance(br, int):
                                dst = logits[:, :, 4 * br + cr:4 * br + cr + 1, :]
                            else:
                                dst = logits[:, :, bass.ds(add(4 * br, cr), 1), :]
                            nc.scalar.copy(dst, misc[:, 0:ST * E].rearrange("p (t b e) -> p t b e", b=1, e=E)
                                           ).then_inc(misc_free, 1)
                        slot(q, c, 1)
                        if live(b3, c3):
                            if has_prior(b3, c3, 1):
                                act.wait_ge(hbo_done, nth(b3, c3, 1, 0))
                            norm_apply(0, b3, c3, xn1, x_in[:, c3 % 2])
                        slot(q, c, 2)
                        if live(b1, c1):
                            act.wait_ge(misc_full, add(misc_use(q, c, "onT"), 1))
                            nc.scalar.copy(onT[:], misc[:, 0:S]).then_inc(misc_free, 1)
                        slot(q, c, 3)
                        slot(q, c, 4)
                        if live(b3, c3):
                            act.wait_ge(misc_full, add(misc_use(q, c, "hT"), 1))
                            nc.scalar.copy(hT[:], misc[:, 0:S]).then_inc(misc_free, 1)
                        slot(q, c, 5)
                        if live(b3, c3):
                            act.wait_ge(misc_full, add(misc_use(q, c, "QK"), 1))
                            if has_prior(b3, c3, 1):
                                pb, pc = batch(b3, c3, -1)
                                act.wait_ge(spread[pc], add(16 * NPROD * pb, 16 * NPROD))
                            else:
                                act.wait_ge(small_loaded, 16 * NSMALL)
                            for n, bias in enumerate((bq_sb, bk_sb)):
                                nc.scalar.activation(qk[:, n], misc[:, n * S:(n + 1) * S], ACT.Identity,
                                                     bias=bias[:]).then_inc((qk_done, misc_free)[n], 1)
                            act.wait_ge(misc_free, add(misc_use(q, c, "QK"), 1))
                            act.wait_ge(qk_done, nth(b3, c3, 1, 1))
                            nc.scalar.copy(qk_part[:, 0::3], qk[:]).then_inc(part0_done, 1)
                        if live(b2, c2):
                            if has_prior(b2, c2, 2):
                                act.wait_ge(xn_stored[c2 % 2], add(32 * b2, 16 * (c2 // 2)))
                            norm_apply(3, b2, c2, xn2[:, c2 % 2], x1[:, c2 % 2])
                        slot(q, c, 6)
                        if live(b3, c3):
                            act.wait_ge(misc_full, add(misc_use(q, c, "V"), 1))
                            if has_prior(b3, c3, 4):
                                act.wait_ge(av_done, nth(b3, c3, 8, -24))
                            else:
                                act.wait_ge(v_done, 3)
                            vd = vst[:, c3].rearrange("p t (g s) c -> p t g (s c)", s=2)
                            src = misc[:, 0:S].rearrange("p (t g s c) -> p t g s c", t=ST, s=2, c=DH)
                            for s2 in range(2):
                                nc.scalar.copy(vd[:, :, :, 48 * s2:48 * s2 + DH], src[:, :, :, s2]).then_inc((v_done, misc_free)[s2], 1)
                        slot(q, c, 7)
                        if live(b3, c3):
                            act.wait_ge(rest_done, nth(b3, c3, 1, 1))
                            nc.scalar.copy(qk_part[:, 1::3], qk_rest[:]).then_inc(part1_done, 1)
                        if on(q, c, B - 4):
                            half0.exponentials(act)

                    steps(act, run)

                @block.vector
                def _(dve):
                    for n in range(NB4):
                        dve.memset(ks_f32[ONES:KROWS, n], PAIR).then_inc(ones_done, 1)
                    dve.wait_ge(v_done, 1)
                    vs = vst[:].rearrange("p b t (g s) c -> p (b t g) s c", s=2)
                    dve.memset(vs[:, :, 0, DH:DH + 1], 1.0).then_inc(v_done, 1)
                    dve.memset(vs[:, :, 1, 16 + DH:16 + DH + 1], 1.0).then_inc(v_done, 1)
                    dve.wait_ge(v_done, 3)
                    dve.wait_ge(small_loaded, 16 * NSMALL)
                    dve.tensor_copy(bv_wide[:], bv_col[:].broadcast_to([P, D])).then_inc(bvo_done, 1)
                    dve.wait_ge(bvo_ps, 1)
                    dve.tensor_tensor(out=bvo[:], in0=misc[:, 0:D], in1=bo_sb[:], op=ALU.add).then_inc(bvo_done, 1)

                    heads16 = misc[:].rearrange("p (h c) -> p h c", c=16)

                    def norm_stats(n, b, c, src):
                        if has_prior(b, c, 1):
                            dve.wait_ge(mv_done[n], nth(b, c, 2, 0))
                        for t in range(ST):
                            dve.bn_stats(out=stats[n][:, t], in_=src[:, t]).then_inc(stats_done[n], 1)

                    def norm_aggr(n, b, c):
                        if has_prior(b, c, 1):
                            dve.wait_ge(norm_done[n], nth(b, c, 2, 0))
                        dve.wait_ge(stats_done[n], nth(b, c, 2, 2))
                        settled(dve)
                        for t in range(ST):
                            dve.bn_aggr(out=mv[n][:, t], in_=stats[n][:, t]).then_inc(mv_done[n], 1)

                    def norm_apply(n, b, c, dst, src):
                        dve.wait_ge(rstd_done[n], nth(b, c, 1, 1))
                        for t in range(ST):
                            dve.tensor_scalar(out=dst[:, t], in0=src[:, t], scalar1=mv[n][:, t, 0:1],
                                              scalar2=rstd[n][:, t:t + 1], op0=ALU.subtract, op1=ALU.mult
                                              ).then_inc(norm_done[n], 1)

                    ROUND_SLOTS = ((B - 2, 15),) + tuple((B - 1, k) for k in (0, 1, 4, 5, 8, 10, 11))

                    def slot_max(q, c, k):
                        b, cc = batch(q, c, 1 if k < 8 else 2)
                        if not live(b, cc):
                            return
                        kk = (k + 8) % 16
                        t, hh = kk // 8, kk % 8 * 2
                        dve.wait_ge(s_done, nth(b, cc, 16, kk + 1))
                        dve.tensor_reduce(out=nm[:, cc % 2, t, hh:hh + 2], in_=ps_s[k % 2][:], axis=AX.X, op=ALU.max,
                                          negate=True).then_inc(max_done, 1)

                    def run(q, c):
                        bm, cm = batch(q, c, 1)
                        b1, c1 = batch(q, c, -1)
                        b2, c2 = batch(q, c, -2)
                        b3, c3 = batch(q, c, 3)
                        b4, c4 = batch(q, c, 4)
                        for k in range(16):
                            if k == 3 and live(b1, c1):
                                dve.wait_ge(misc_full, add(misc_use(q, c, "OT"), 1))
                                dve.reciprocal(o_rec[:], heads16[:, :, DH]).then_inc(orec_done, 1)
                            if k == 12 and live(bm, cm):
                                dve.wait_ge(misc_full, add(misc_use(q, c, "nmT"), 1))
                                if has_prior(bm, cm, 1):
                                    pb, pc = batch(bm, cm, -1)
                                    dve.wait_ge(nm_spread[pc], add(16 * pb, 16))
                                dve.tensor_copy(nmT[:], misc[0:3 * H, 0:S // 2].bitcast(BF16)).then_inc(misc_free, 1)
                            if k == 7 and live(b1, c1):
                                dve.wait_ge(misc_full, add(misc_use(q, c, "Wo"), 1))
                                dve.wait_ge(hbo_done, nth(b1, c1, 1, 1))
                                dve.tensor_tensor(out=y[:], in0=misc[:, 0:S].rearrange("p (t d) -> p t d", d=D),
                                                  in1=h_bo[:, c1], op=ALU.add).then_inc(misc_free, 1)
                            if k == 7 and live(b2, c2):
                                norm_aggr(3, b2, c2)
                            slot_max(q, c, k)
                            if k == 0 and live(b2, c2):
                                dve.wait_ge(bet_done, nth(b2, c2, 2, 2))
                                norm_stats(2, b2, c2, z2b)
                            if k == 1 and live(b2, c2):
                                norm_aggr(2, b2, c2)
                            if k == 3 and live(b1, c1):
                                dve.wait_ge(orec_done, nth(b1, c1, 1, 1))
                                dve.tensor_tensor(out=o_norm[:].rearrange("p t (h c) -> p (t h) c", c=DH), in0=heads16[:, :, 0:DH],
                                                  in1=o_rec[:].rearrange("p (h a) -> p h a", a=1).broadcast_to([P, ST * H, DH]),
                                                  op=ALU.mult).then_inc(misc_free, 1)
                            if k == 4 and live(b2, c2):
                                if has_prior(b2, c2, 1):
                                    dve.wait_ge(x1_done, nth(b2, c2, 1, 0))
                                norm_apply(2, b2, c2, z3, z2b)
                            if k == 6 and live(b2, c2):
                                dve.wait_ge(x1_done, nth(b2, c2, 1, 1))
                                norm_stats(3, b2, c2, x1[:, c2 % 2])
                            if k == 8 and live(b1, c1):
                                dve.wait_ge(misc_free, add(misc_use(q, c, "Wo"), 1))
                                norm_stats(1, b1, c1, y)
                            if k == 9 and live(b1, c1):
                                norm_aggr(1, b1, c1)
                            if k == 12 and live(b1, c1):
                                norm_apply(1, b1, c1, z2, y)
                            if k == 14 and on(q, c, B - 4):
                                qr, cr = divmod(RB - 1 + 3, 4)
                                dve.wait_ge(misc_free, misc_use(qr, cr, "logit") + 1)
                                half0.less_max(dve)
                            if k == 8 and on(q, c, B - 2):
                                half0.over_sum(dve)
                            if k == 14 and on(q, c, B - 2):
                                dve.wait_ge(aff_ps, 1)
                                dve.tensor_copy(scan[:], ps_s[0][:, 0]).then_inc(top_done, 1)
                            if isinstance(q, int) and (4 * q + c, k) in ROUND_SLOTS:
                                n = ROUND_SLOTS.index((4 * q + c, k))
                                top_round(dve, top_done, 3 * n + 1, n, scan[:], top_gate, top_idx)
                            if k == 13 and on(q, c, B - 1):
                                top_copies(dve, top_done, 3 * ROUNDS + 1, top_gate, top_idx, top_token)
                            if k == 15 and on(q, c, B):
                                dve.wait_ge(top_ps, 1)
                                slot_copies(dve, slots_done, 0, ps_s[1][:, :, 0:P])
                            if k == 14 and live(b4, c4):
                                dve.wait_ge(x_loaded[c4 % 2], add(32 * b4, 16 * (c4 // 2) + 16))
                                norm_stats(0, b4, c4, x_in[:, c4 % 2])
                            if k == 15 and live(b4, c4):
                                norm_aggr(0, b4, c4)

                    steps(dve, run)

                @block.tensor
                def _(pe):
                    pe.wait_ge(consts, 5)
                    pe.wait_ge(small_loaded, 16 * NSMALL)
                    pe.wait_ge(bvo_done, 1)
                    nc.tensor.matmul(misc[:, 0:D], bv_wide[:], wo_sb[:], start=True, stop=True).then_inc(bvo_ps, 1)
                    pe.wait_ge(bvo_done, 2)

                    def slot_scores(q, c, k):
                        b, cc = batch(q, c, 1 if k < 8 else 2)
                        if not live(b, cc):
                            return
                        kk = (k + 8) % 16
                        t, hh = kk // 8, kk % 8 * 2
                        if kk == 0:
                            pe.wait_ge(spread[cc], add(16 * NPROD * b, 16 * NPROD))
                        if kk >= 2 or has_prior(b, cc, 1):
                            pe.wait_ge(max_done, nth(b, cc, 16, kk - 1))
                        for n in range(2):
                            last = nc.tensor.matmul(ps_s[k % 2][:, n], qs[0:MROW, cc, hh + n, t * P:(t + 1) * P],
                                                    ks[0:MROW, cc, hh + n, :], start=True, stop=True)
                        last.then_inc(s_done, 1)

                    def heads(u):
                        j, s2, kt = u // 4, u // 2 % 2, u % 2
                        return j, s2, kt, [8 * j + 2 * g + s2 for g in range(4)]

                    def slot_st(q, c, u):
                        if not live(q, c):
                            return
                        j, s2, kt, hs = heads(u)
                        if u == 0:
                            pe.wait_ge(nm_spread[c], add(16 * q, 16))
                        if u >= 2 or has_prior(q, c, 1):
                            pe.wait_ge(exp_done, nth(q, c, 8, u - 1))
                        for g, hd in enumerate(hs):
                            last = nc.tensor.matmul(ps_st[u % 2][:, g], ks[0:KROWS, c, hd, kt * P:(kt + 1) * P],
                                                    qs[0:KROWS, c, hd, :], start=True, stop=True)
                        last.then_inc(st_done, 1)

                    def slot_av(q, c, u):
                        if not live(q, c):
                            return
                        j, s2, kt, hs = heads(u)
                        pe.wait_ge(exp_done, nth(q, c, 8, u + 1))
                        if u == 0:
                            if has_prior(q, c, 1):
                                pe.wait_ge(oaug_done, nth(q, c, 1, 0))
                        for g, hd in enumerate(hs):
                            last = nc.tensor.matmul(ps_av[32 * g:32 * g + 32, j], vst[:, c, kt, hd], probs[:, u % 4, g],
                                                    start=(s2 == 0 and kt == 0), stop=(s2 == 1 and kt == 1))
                        last.then_inc(av_done, 1)

                    def free(q, c, name):
                        n = misc_use(q, c, name)
                        if not isinstance(n, int) or n > 0:
                            pe.wait_ge(misc_free, n)

                    def run(q, c):
                        bm, cm = batch(q, c, 1)
                        b1, c1 = batch(q, c, -1)
                        b2, c2 = batch(q, c, -2)
                        b3, c3 = batch(q, c, 3)
                        br, cr = batch(q, c, -3)
                        if isinstance(q, int) and 4 * q + c == WARM_STEP:
                            free(q, c, "OT")
                            for n in range(WARM):
                                nc.tensor.matmul(misc[:, 0:P], ident[:], ident[:], start=True, stop=True)
                        if live(br, cr):
                            pe.wait_ge(norm_done[3], nth(br, cr, 2, 2))
                            free(q, c, "xnT")
                            for t in range(ST):
                                last = nc.tensor.transpose(misc[:, t * P:(t + 1) * P], xn2[:, cr % 2, t], ident[:])
                            last.then_inc(misc_full, 1)
                        for k in range(16):
                            u = k // 2
                            if k % 2 == 0:
                                slot_st(q, c, u)
                            if k == 10 and live(b3, c3):
                                free(q, c, "QK")
                                for n, w in enumerate((wq_sb, wk_sb)):
                                    last = nc.tensor.matmul(misc[:, n * S:(n + 1) * S], w[:], hT[:], start=True, stop=True)
                                last.then_inc(misc_full, 1)
                            slot_scores(q, c, k)
                            if k == 12 and live(bm, cm):
                                pe.wait_ge(nm2_done, nth(bm, cm, 1, 1))
                                free(q, c, "nmT")
                                settled(pe)
                                for t in range(ST):
                                    last = nc.tensor.transpose(misc[0:3 * H, t * P // 2:(t + 1) * P // 2].bitcast(BF16),
                                                               nm_part[:, t].rearrange("p a h -> p (a h)"), identb[:])
                                last.then_inc(misc_full, 1)
                            if k % 2 == 0:
                                if u:
                                    slot_av(q, c, u - 1)
                                else:
                                    slot_av(b1, c1, 7)
                            if k == 1 and live(br, cr):
                                free(q, c, "logit")
                                for t in range(ST):
                                    last = nc.tensor.matmul(misc[:, t * E:(t + 1) * E], xnT[:, t * P:(t + 1) * P],
                                                            gate_sb[:], start=True, stop=True)
                                last.then_inc(misc_full, 1)
                            if k == 2 and live(b1, c1):
                                pe.wait_ge(oaug_done, nth(b1, c1, 1, 1))
                                free(q, c, "OT")
                                for t in range(ST):
                                    for j in range(2):
                                        last = nc.tensor.transpose(misc[:, (2 * t + j) * P:(2 * t + j + 1) * P],
                                                                   o_aug[:, j, t * P:(t + 1) * P], ident[:])
                                last.then_inc(misc_full, 1)
                            if k == 5 and live(b1, c1):
                                free(q, c, "onT")
                                for t in range(ST):
                                    last = nc.tensor.transpose(misc[:, t * P:(t + 1) * P], o_norm[:, t], ident[:])
                                last.then_inc(misc_full, 1)
                            if k == 6 and live(b1, c1):
                                free(q, c, "Wo")
                                for t in range(ST):
                                    last = nc.tensor.matmul(misc[:, t * D:(t + 1) * D], onT[:, t * P:(t + 1) * P], wo_sb[:],
                                                            start=True, stop=True)
                                last.then_inc(misc_full, 1)
                            if k == 8 and live(b3, c3):
                                pe.wait_ge(h_done, nth(b3, c3, 1, 1))
                                free(q, c, "hT")
                                for t in range(ST):
                                    last = nc.tensor.transpose(misc[:, t * P:(t + 1) * P], h[:, c3 % 2, t], ident[:])
                                last.then_inc(misc_full, 1)
                            if k == 13 and live(b3, c3):
                                free(q, c, "V")
                                for t in range(ST):
                                    last = nc.tensor.matmul(misc[:, t * D:(t + 1) * D], hT[:, t * P:(t + 1) * P], wv_sb[:],
                                                            start=True, stop=True)
                                last.then_inc(misc_full, 1)
                            if k == 14 and on(q, c, B - 2):
                                pe.wait_ge(max_done, 16 * B)
                                half0.transposed(pe, ps_s[0][:, 0], aff_ps)
                            if k == 15 and on(q, c, B):
                                pe.wait_ge(top_done, 3 * ROUNDS + 4)
                                for n, src in enumerate((top_token, top_gate)):
                                    last = nc.tensor.transpose(ps_s[1][:, n, 0:P], src[:].rearrange("p a j -> p (a j)"), ident[:])
                                last.then_inc(top_ps, 1)

                    steps(pe, run)

        w_hi = [sb(f"w_hi{n}", [P, E, I], F32R) for n in range(2)]
        w_lo = [sb(f"w_lo{n}", [P, E, I], F32R) for n in range(2)]

        wh_done, wl_done = sem("wh_done"), sem("wl_done")

        def first_part(e, which):
            nc.scalar.copy(w_hi[which][:, e:e + 2], (wg_sb, wu_sb)[which][:, e:e + 2]).then_inc(wh_done, 1)

        def split_weights(eng, e, which):
            lo, hi, w = w_lo[which], w_hi[which], (wg_sb, wu_sb)[which]
            eng.wait_ge(wh_done, e + which + 1)
            eng.tensor_tensor(out=lo[:, e:e + 2], in0=w[:, e:e + 2], in1=hi[:, e:e + 2], op=ALU.subtract).then_inc(wl_done, 1)

        with ExitStack() as rctx:
            half1 = Half(1, lambda name, shape: sb(name, shape, F32, rctx))
            ps_aff = ps("ps_aff", [P, S], F32, rctx)
            r_aff, r_scan = sem("r_aff"), sem("r_scan")

            with nc.Block() as block:
                @block.vector
                def _(dve):
                    half1.less_max(dve)
                    half1.over_sum(dve)
                    dve.wait_ge(r_aff, 1)
                    dve.tensor_copy(scan_late, ps_aff[:]).then_inc(r_scan, 1)
                    split_weights(dve, 0, 1)

                @block.scalar
                def _(act):
                    act.wait_ge(w_loaded, 48 * E)
                    for which in range(2):
                        first_part(0, which)
                    half1.exponentials(act)

                @block.gpsimd
                def _(pool):
                    split_weights(pool, 0, 0)

                @block.tensor
                def _(pe):
                    half1.transposed(pe, ps_aff, r_aff)

        with ExitStack() as ectx:
            def se(name, shape, dt=F32):
                return sb(name, shape, dt, ectx)

            NBX = 4
            NU = E * IT
            tok_pick = se("tok_pick", [P, GB, M])
            tok_put = se("tok_put", [P, GB, M])
            gat = se("gat", [P, GB, M])
            xn_rows = se("xn_rows", [P, NBX, ST, D])
            xn_hi = se("xn_hi", [P, 2, ST, D], F32R)
            xn_lo = se("xn_lo", [P, 2, ST, D], F32R)
            x1_rows = se("x1_rows", [P, NBX, ST, D])
            pick = se("pick", [P, 2, M, S], BF16)
            pickT = se("pickT", [P, 2, ST, M * P], F32R)
            xeT_hi = se("xeT_hi", [P, E, GB * CAP], F32R)
            xeT_lo = se("xeT_lo", [P, E, GB * CAP], F32R)
            silu = se("silu", [P, 2, GB * CAP])
            NBH = 3
            hid = se("hid", [P, NBH, IT, GB * CAP])
            put = wg_sb[:].rearrange("p e i -> p (e i)").rearrange("p (b m s) -> p b m s", b=NBX, m=M)
            xe = wu_sb[:].rearrange("p e i -> p (e i)").rearrange("p (m b d) -> p m b d", m=M, b=GB)
            est = se("est", [P, 2, ST, 6])
            emv = se("emv", [P, 2, ST, 2])
            eve = se("eve", [P, ST])
            negm = se("negm", [P, ST])
            ers = se("ers", [P, 2, ST])
            nmr = se("nmr", [P, 2, ST])
            zn = se("zn", [P, 2, ST, D])
            res = se("res", [P, 2, ST, D])

            ps_g = [ps(f"ps_g{n}", [P, GB * CAP], F32, ectx) for n in range(2)]
            ps_u = [ps(f"ps_u{n}", [P, GB * CAP], F32, ectx) for n in range(2)]
            ps_d = ps("ps_d", [P, GB, D], F32, ectx)
            ps_p = ps("ps_p", [P, ST, M * P], BF16, ectx)
            ps_x = ps("ps_x", [P, ST, D], F32, ectx)
            ps_pt = (ps_p[:], ps_d[:, GB // 2:].rearrange("p b d -> p (b d)").bitcast(BF16).rearrange("p (t n) -> p t n", t=ST))
            ps_f = (ps_x[:], ps_d[:, 0:ST])
            ps_fl = ps_f + tuple(t[:].rearrange("p (t d) -> p t d", t=GB // 2)[:, 0:ST] for t in (ps_g[0], ps_u[0]))

            def sum_bank(b, follows):
                return ps_f[b % 2] if follows else ps_fl[b % 4]

            xn_loaded = [sem(f"xn_loaded{n}") for n in range(NBX)]
            x1_loaded = [sem(f"x1_loaded{n}") for n in range(NBX)]
            hi_done, lo_done = sem("hi_done"), sem("lo_done")
            tok_done = sem("tok_done")
            pick_done, pickT_ps, pickT_done = sem("pick_done"), sem("pickT_ps"), sem("pickT_done")
            ghi_ps, glo_ps, xehi_done, xelo_done = sem("ghi_ps"), sem("glo_ps"), sem("xehi_done"), sem("xelo_done")
            g_ps, u_ps, silu_done, hid_done = sem("g_ps"), sem("u_ps"), sem("silu_done"), sem("hid_done")
            down_ps, xe_done = sem("down_ps"), sem("xe_done")
            put_done, f_ps, est_done, eve_done, negm_done, ers_done = (
                sem(n) for n in ("put_done", "f_ps", "est_done", "eve_done", "negm_done", "ers_done"))
            emv_done, nmr_done, zn_done, res_done = (sem(n) for n in ("emv_done", "nmr_done", "zn_done", "res_done"))
            stored = [sem(f"stored{n}") for n in range(2)]
            late_top, late_ps, late_slots = sem("late_top"), sem("late_ps"), sem("late_slots")
            LATE_ROUNDS = (2, 4, 6, 7, 9, 14, 16, 17)
            LATE_COPIES, LATE_PS, LATE_SLOTS = 20, 24, 26

            def first(g):
                return isinstance(g, int) and g == 0

            def val(k, g, m):
                return add(k * g, m)

            def groups(eng, prologue, body):
                prologue()
                body(0, True)
                with eng.Fori(1, NG - 1) as g:
                    body(g, True)
                body(NG - 1, False)

            def rows_of(t, g, b):
                i = val(GB, g, b)
                v = t[i:i + 1] if isinstance(i, int) else t[bass.ds(i, 1)]
                return v.rearrange("b p t d -> (b p) t d")

            with nc.Block() as block:
                @block.sync
                def _(sp):
                    def load_xn(g, b):
                        if not isinstance(g, int) or g > 0 or b >= NBX:
                            sp.wait_ge(lo_done, val(GB, g, b - NBX + 1))
                            settled(sp)
                        sp.dma_start(xn_rows[:, b % NBX], rows_of(xn_dram, g, b)).then_inc(xn_loaded[b % NBX], 16)

                    def load_x1(g, b):
                        sp.wait_ge(res_done, val(GB, g, max(b - NBX + 1, 0) + 1))
                        settled(sp)
                        sp.dma_start(x1_rows[:, b % NBX], rows_of(x1_dram, g, b)).then_inc(x1_loaded[b % NBX], 16)

                    def prologue():
                        for n in range(2):
                            sp.sem_inc(stored[n], 1)
                        for b in range(GB):
                            load_xn(0, b)

                    def body(g, follows):
                        for b in range(NBX):
                            load_x1(g, b)
                        if follows:
                            for b in range(NBX + 1):
                                load_xn(g + 1, b)
                        for b in range(GB):
                            if follows and b + NBX + 1 < GB:
                                load_xn(g + 1, b + NBX + 1)
                            sp.wait_ge(res_done, val(GB, g, b + 2))
                            settled(sp)
                            i = val(GB, g, b)
                            dst = out[i:i + 1] if isinstance(i, int) else out[bass.ds(i, 1)]
                            sp.dma_start(dst.rearrange("b (t p) d -> (b p) t d", p=P), res[:, b % 2]).then_inc(stored[b % 2], 16)
                            if b + NBX < GB:
                                load_x1(g, b + NBX)

                    groups(sp, prologue, body)
                    for n in range(2):
                        sp.wait_ge(stored[n], 16 * (B // 2) + 1)

                @block.gpsimd
                def _(pool):
                    def split_lo(g, b):
                        pool.wait_ge(hi_done, val(GB, g, b + 1))
                        pool.tensor_tensor(out=xn_lo[:, b % 2], in0=xn_rows[:, b % NBX], in1=xn_hi[:, b % 2], op=ALU.subtract
                                           ).then_inc(lo_done, 1)

                    def rstd_of(g, b):
                        pool.wait_ge(nmr_done, val(GB, g, b + 1))
                        pool.wait_ge(emv_done, val(2 * GB, g, 2 * b + 3))
                        settled(pool)
                        pool.tensor_scalar(out=eve[:], in0=emv[:, b % 2, :, 1], scalar1=EPS, scalar2=None, op0=ALU.add).then_inc(eve_done, 1)
                        pool.tensor_scalar(out=negm[:], in0=emv[:, b % 2, :, 0], scalar1=-1.0, scalar2=None, op0=ALU.mult).then_inc(negm_done, 1)
                        pool.wait_ge(zn_done, val(2 * GB, g, 2 * max(b - 1, 0) + 1))
                        pool.wait_ge(eve_done, val(GB, g, b + 1))
                        pool.tensor_tensor(out=ers[:, b % 2], in0=eve[:], in1=neghalf[:], op=ALU.pow).then_inc(ers_done, 1)
                        pool.wait_ge(negm_done, val(GB, g, b + 1))
                        pool.wait_ge(ers_done, val(GB, g, b + 1))
                        pool.tensor_tensor(out=nmr[:, b % 2], in0=negm[:], in1=ers[:, b % 2], op=ALU.mult).then_inc(nmr_done, 1)

                    def residual(g, b):
                        pool.wait_ge(zn_done, val(2 * GB, g, 2 * b + 3))
                        pool.wait_ge(x1_loaded[b % NBX], val(16 * GB // NBX, g, 16 * (b // NBX) + 16))
                        pool.wait_ge(stored[b % 2], val(16 * GB // 2, g, 16 * (b // 2) + 1))
                        pool.tensor_tensor(out=res[:, b % 2], in0=zn[:, b % 2], in1=x1_rows[:, b % NBX], op=ALU.add).then_inc(res_done, 1)

                    def prologue():
                        for one in (nmr_done, res_done):
                            pool.sem_inc(one, 1)
                        for b in range(GB):
                            split_lo(0, b)

                    def body(g, follows):
                        if first(g):
                            for e in range(2, E, 2):
                                for which in range(2):
                                    split_weights(pool, e, which)
                        if follows:
                            for b in range(2):
                                split_lo(g + 1, b)
                        for b in range(GB):
                            if follows and b + 2 < GB:
                                split_lo(g + 1, b + 2)
                            rstd_of(g, b)
                            if b:
                                residual(g, b - 1)
                        residual(g, GB - 1)

                    groups(pool, prologue, body)

                @block.scalar
                def _(act):
                    def split_hi(g, b):
                        act.wait_ge(xn_loaded[b % NBX], val(16 * GB // NBX, g, 16 * (b // NBX) + 16))
                        if not isinstance(g, int) or g > 0 or b >= 2:
                            act.wait_ge(glo_ps, val(GB, g, b - 1))
                        nc.scalar.copy(xn_hi[:, b % 2], xn_rows[:, b % NBX]).then_inc(hi_done, 1)

                    def copy_pick(g, b):
                        act.wait_ge(pickT_ps, val(GB, g, b + 1))
                        if not isinstance(g, int) or g > 0 or b >= 2:
                            act.wait_ge(glo_ps, val(GB, g, b - 1))
                        nc.scalar.copy(pickT[:, b % 2], ps_pt[b % 2]).then_inc(pickT_done, 1)

                    def gathered_hi(g, b):
                        act.wait_ge(ghi_ps, val(GB, g, b + 1))
                        nc.scalar.copy(xeT_hi[:, :, b * CAP:(b + 1) * CAP], ps_g[b % 2][:].rearrange("p (e j) -> p e j", e=E)
                                       ).then_inc(xehi_done, 1)

                    def last_norm(g, b, follows):
                        act.wait_ge(nmr_done, val(GB, g, b + 2))
                        act.wait_ge(res_done, val(GB, g, max(b - 1, 0) + 1))
                        for t in range(ST):
                            nc.scalar.activation(zn[:, b % 2, t], sum_bank(b, follows)[:, t], ACT.Identity, bias=nmr[:, b % 2, t:t + 1],
                                                 scale=ers[:, b % 2, t:t + 1]).then_inc(zn_done, 1)

                    def gated(g, n):
                        act.wait_ge(g_ps, val(NU, g, n + 1))
                        if n >= 2 or not isinstance(g, int) or g > 0:
                            act.wait_ge(hid_done, val(NU, g, n - 1))
                        nc.scalar.activation(silu[:, n % 2], ps_g[n % 2][:], ACT.Silu).then_inc(silu_done, 1)

                    def prologue():
                        act.sem_inc(zn_done, 1)
                        for b in range(2):
                            split_hi(0, b)
                        copy_pick(0, 0)
                        for b in range(GB):
                            if b + 1 < GB:
                                copy_pick(0, b + 1)
                            gathered_hi(0, b)
                            if b + 2 < GB:
                                split_hi(0, b + 2)
                        for n in range(2):
                            gated(0, n)

                    def body(g, follows):
                        for n in range(2, NU):
                            gated(g, n)
                            if first(g) and n < E:
                                first_part(n // 2 * 2, n % 2)
                        if follows:
                            for b in range(2):
                                split_hi(g + 1, b)
                            copy_pick(g + 1, 0)
                        for b in range(GB):
                            if follows:
                                if b + 1 < GB:
                                    copy_pick(g + 1, b + 1)
                                gathered_hi(g + 1, b)
                                if b + 2 < GB:
                                    split_hi(g + 1, b + 2)
                            if b:
                                last_norm(g, b - 1, follows)
                        if follows:
                            for n in range(2):
                                gated(g + 1, n)
                        last_norm(g, GB - 1, follows)

                    groups(act, prologue, body)

                @block.vector
                def _(dve):
                    def copy_tokens(dst, src, g):
                        i = GB * g
                        v = src[:, i:i + GB] if isinstance(g, int) else src[:, bass.ds(i, GB)]
                        dve.tensor_copy(dst[:], v).then_inc(tok_done, 1)

                    def one_hot(dst, tok, b, done):
                        for m in range(M):
                            dve.tensor_scalar(out=dst[:, m], in0=iota[:], scalar1=tok[:, b, m:m + 1], scalar2=None,
                                              op0=ALU.is_equal).then_inc(done, 1)

                    def pick_rows(g, b):
                        if not isinstance(g, int) or g > 0 or b >= 2:
                            dve.wait_ge(pickT_ps, val(GB, g, b - 1))
                        one_hot(pick[:, b % 2], tok_pick, b, pick_done)

                    def put_rows(g, b):
                        if b >= NBX:
                            dve.wait_ge(f_ps, val(GB, g, b - NBX + 1))
                        one_hot(put[:, b % NBX], tok_put, b, put_done)

                    def gathered_lo(g, b):
                        dve.wait_ge(glo_ps, val(GB, g, b + 1))
                        dve.tensor_copy(xeT_lo[:, :, b * CAP:(b + 1) * CAP], ps_u[b % 2][:].rearrange("p (e j) -> p e j", e=E)
                                        ).then_inc(xelo_done, 1)

                    def last_stats(g, b, follows):
                        dve.wait_ge(emv_done, val(2 * GB, g, 2 * max(b - 1, 0) + 1))
                        dve.wait_ge(f_ps, val(GB, g, b + 1))
                        for t in range(ST):
                            dve.bn_stats(out=est[:, b % 2, t], in_=sum_bank(b, follows)[:, t]).then_inc(est_done, 1)

                    def last_aggr(g, b):
                        dve.wait_ge(est_done, val(2 * GB, g, 2 * b + 2))
                        dve.wait_ge(nmr_done, val(GB, g, max(b - 1, 0) + 1))
                        settled(dve)
                        for t in range(ST):
                            dve.bn_aggr(out=emv[:, b % 2, t], in_=est[:, b % 2, t]).then_inc(emv_done, 1)

                    def weighted(g, m, n):
                        bs = slice(n * GB // 2, (n + 1) * GB // 2)
                        dve.wait_ge(down_ps, val(2 * M, g, 2 * m + n + 1))
                        dve.tensor_tensor(out=xe[:, m, bs], in0=ps_d[:, bs], in1=gat[:, bs, m:m + 1].broadcast_to([P, GB // 2, D]),
                                          op=ALU.mult).then_inc(xe_done, 1)

                    def prologue():
                        dve.sem_inc(emv_done, 1)
                        copy_tokens(tok_pick, slot_token, 0)
                        dve.wait_ge(tok_done, 1)
                        for b in range(2):
                            pick_rows(0, b)
                        for b in range(GB):
                            if b + 2 < GB:
                                pick_rows(0, b + 2)
                            gathered_lo(0, b)

                    def body(g, follows):
                        copy_tokens(tok_put, slot_token, g)
                        copy_tokens(gat, slot_gate, g)
                        dve.wait_ge(tok_done, val(3, g, 3))
                        for n in range(NU):
                            e, it = n // IT, n % IT
                            dve.wait_ge(silu_done, val(NU, g, n + 1))
                            dve.wait_ge(u_ps, val(NU, g, n + 1))
                            if e >= NBH and it == 0:
                                dve.wait_ge(down_ps, val(2 * M, g, (e - NBH) // 2 * 2 + 2))
                            dve.tensor_tensor(out=hid[:, e % NBH, it], in0=silu[:, n % 2], in1=ps_u[n % 2][:], op=ALU.mult
                                              ).then_inc(hid_done, 1)
                            if n % (2 * IT) in (2, 3) and n > IT:
                                weighted(g, n // (2 * IT) - 1, n % 2)
                            if n % (2 * IT) == 1:
                                if first(g):
                                    dve.wait_ge(wl_done, e // 2 * 2 + 2)
                                put_rows(g, n // (2 * IT))
                            if first(g) and n in LATE_ROUNDS:
                                i = LATE_ROUNDS.index(n)
                                top_round(dve, late_top, 3 * i, i, scan_late, top_gate_late, top_idx_late)
                            if first(g) and n == LATE_COPIES:
                                top_copies(dve, late_top, 3 * ROUNDS, top_gate_late, top_idx_late, top_token_late)
                            if first(g) and n == LATE_SLOTS:
                                dve.wait_ge(late_ps, 1)
                                slot_copies(dve, late_slots, 1, ps_x)
                                dve.wait_ge(late_slots, 4)
                            if n == NU - 16 and follows:
                                copy_tokens(tok_pick, slot_token, g + 1)
                            if n == NU - 15 and follows:
                                dve.wait_ge(tok_done, val(3, g, 4))
                                pick_rows(g + 1, 0)
                            if n == NU - 7 and follows:
                                pick_rows(g + 1, 1)
                        for n in range(2):
                            weighted(g, M - 1, n)
                        for b in range(GB):
                            if follows:
                                if b + 2 < GB:
                                    pick_rows(g + 1, b + 2)
                                gathered_lo(g + 1, b)
                            last_stats(g, b, follows)
                            if b + NBX < GB:
                                put_rows(g, b + NBX)
                            last_aggr(g, b)

                    groups(dve, prologue, body)

                @block.tensor
                def _(pe):
                    def transpose_pick(g, b):
                        pe.wait_ge(pick_done, val(GB * M, g, M * (b + 1)))
                        if not isinstance(g, int) or g > 0 or b >= 2:
                            pe.wait_ge(pickT_done, val(GB, g, b - 1))
                        for t in range(ST):
                            for m in range(M):
                                last = nc.tensor.transpose(ps_pt[b % 2][:, t, m * P:(m + 1) * P],
                                                           pick[:, b % 2, m, t * P:(t + 1) * P], identb[:])
                        last.then_inc(pickT_ps, 1)

                    def gather(g, b):
                        pe.wait_ge(pickT_done, val(GB, g, b + 1))
                        pe.wait_ge(lo_done, val(GB, g, b + 1))
                        if not isinstance(g, int) or g > 0 or b >= 2:
                            pe.wait_ge(xehi_done, val(GB, g, b - 1))
                            pe.wait_ge(xelo_done, val(GB, g, b - 1))
                        for bank, part, done in ((ps_g, xn_hi, ghi_ps), (ps_u, xn_lo, glo_ps)):
                            for t in range(ST):
                                last = nc.tensor.matmul(bank[b % 2][:], part[:, b % 2, t], pickT[:, b % 2, t],
                                                        start=t == 0, stop=t == ST - 1)
                            last.then_inc(done, 1)

                    def gate_up(g, n):
                        e, it = n // IT, n % IT
                        if first(g) and n % (2 * IT) == 0:
                            pe.wait_ge(wl_done, e + 2)
                        if n >= 2:
                            pe.wait_ge(hid_done, val(NU, g, n - 1))
                        for k, (bank, done) in enumerate(((ps_g, g_ps), (ps_u, u_ps))):
                            hi, lo = (w[k][:, e, it * P:(it + 1) * P] for w in (w_hi, w_lo))
                            nc.tensor.matmul(bank[n % 2][:], hi, xeT_hi[:, e], start=True, stop=False)
                            nc.tensor.matmul(bank[n % 2][:], hi, xeT_lo[:, e], start=False, stop=False)
                            nc.tensor.matmul(bank[n % 2][:], lo, xeT_hi[:, e], start=False, stop=True).then_inc(done, 1)

                    def down(g, m):
                        pe.wait_ge(hid_done, val(NU, g, 2 * IT * (m + 1)))
                        if not m:
                            pe.wait_ge(zn_done, val(2 * GB, g, 1))
                        for b in range(GB):
                            if m and b % (GB // 2) == 0:
                                pe.wait_ge(xe_done, val(2 * M, g, 2 * m - 1 + b // (GB // 2)))
                            for it in range(IT):
                                for half in range(2):
                                    last = nc.tensor.matmul(ps_d[half * CAP:(half + 1) * CAP, b],
                                                            hid[:, (2 * m + half) % NBH, it, b * CAP:(b + 1) * CAP],
                                                            wd_sb[:, 2 * m + half, it],
                                                            start=it == 0, stop=it == IT - 1)
                            if b % (GB // 2) == GB // 2 - 1:
                                last.then_inc(down_ps, 1)

                    def scatter(g, b, follows):
                        pe.wait_ge(put_done, val(GB * M, g, M * (b + 1)))
                        n = 2 if follows else 4
                        if b >= n:
                            pe.wait_ge(zn_done, val(2 * GB, g, 2 * (b - n) + 3))
                        for t in range(ST):
                            for m in range(M):
                                last = nc.tensor.matmul(sum_bank(b, follows)[:, t], put[:, b % NBX, m, t * P:(t + 1) * P],
                                                        xe[:, m, b], start=m == 0, stop=m == M - 1)
                        last.then_inc(f_ps, 1)

                    def prologue():
                        transpose_pick(0, 0)
                        for b in range(GB):
                            if b + 1 < GB:
                                transpose_pick(0, b + 1)
                            gather(0, b)

                    def body(g, follows):
                        pe.wait_ge(xehi_done, val(GB, g, GB))
                        pe.wait_ge(xelo_done, val(GB, g, GB))
                        for n in range(NU):
                            gate_up(g, n)
                            if first(g) and n == LATE_PS:
                                pe.wait_ge(late_top, 3 * ROUNDS + 3)
                                for k, src in enumerate((top_token_late, top_gate_late)):
                                    last = nc.tensor.transpose(ps_x[:, k], src[:].rearrange("p a j -> p (a j)"), ident[:])
                                last.then_inc(late_ps, 1)
                            if n % (2 * IT) == 1 and n > IT:
                                down(g, n // (2 * IT) - 1)
                        if follows:
                            transpose_pick(g + 1, 0)
                        down(g, M - 1)
                        if follows:
                            gather(g + 1, 0)
                        pe.wait_ge(xe_done, val(2 * M, g, 2 * M))
                        for b in range(GB):
                            if follows and b:
                                gather(g + 1, b)
                            if follows and b + 1 < GB:
                                transpose_pick(g + 1, b + 1)
                            scatter(g, b, follows)

                    groups(pe, prologue, body)


def kernel(**inputs):
    import numpy as np
    import concourse.bacc as bacc
    from concourse import mybir as mb
    from concourse.bass_utils import run_bass_kernel_spmd

    a = {n.split("_", 1)[1]: np.asarray(v) for n, v in inputs.items()}

    def by_lane(w):
        return w.reshape(*w.shape[:-1], H, DH).swapaxes(-1, -2).reshape(w.shape)

    pos = np.arange(S, dtype=np.float32)[:, None]
    div = np.exp(np.arange(0, D, 2, dtype=np.float32) * np.float32(-np.log(10000.0) / D))
    pe_tab = np.zeros((S, D), np.float32)
    pe_tab[:, 0::2] = np.sin(pos * div)
    pe_tab[:, 1::2] = np.cos(pos * div)
    arrays = {
        "x": a["attn_x"], "Wq": by_lane(a["attn_Wq"]), "bq": by_lane(a["attn_bq"]), "Wk": by_lane(a["attn_Wk"]),
        "bk": by_lane(a["attn_bk"]), "Wv": a["attn_Wv"], "bv": a["attn_bv"], "Wo": a["attn_Wo"], "bo": a["attn_bo"],
        "gamma": a["attn_gamma"], "beta": a["attn_beta"], "gate": a["ffn_gate_w"].T,
        "wg": a["ffn_w_gate"].transpose(0, 2, 1), "wu": a["ffn_w_up"].transpose(0, 2, 1),
        "wd": a["ffn_w_down"].transpose(0, 2, 1), "pe_tab": pe_tab,
    }
    arrays = {n: np.ascontiguousarray(v) for n, v in arrays.items()}
    nc = bacc.Bacc("TRN2", target_bir_lowering=False, num_devices=1)
    args = [nc.dram_tensor(n, v.shape, mb.dt.from_np(v.dtype), kind="ExternalInput").ap() for n, v in arrays.items()]
    out = nc.dram_tensor("out", (B, S, D), mb.dt.float32, kind="ExternalOutput").ap()
    build(nc, *args, out)
    r = run_bass_kernel_spmd(nc, [arrays], core_ids=[0])
    return r.results[0]["out"]
```
